# Optimizing a Trainium2 kernel written in Bass

```python
import numpy as np
import jax
import jax.numpy as jnp

def _softmax(x, axis=-1):
    return jax.nn.softmax(x, axis=axis)

def _gelu(x):
    return jax.nn.gelu(x, approximate=True)

def _silu(x):
    return jax.nn.silu(x)

def _sigmoid(x):
    return jax.nn.sigmoid(x)

def _layernorm(x, axis=-1, eps=1e-05):
    m = jnp.mean(x, axis=axis, keepdims=True)
    v = jnp.var(x, axis=axis, keepdims=True)
    return (x - m) / jnp.sqrt(v + eps)

def _scatter_add(tgt, idx, src, axis=0):
    return tgt.at[idx].add(src)

def _segment_sum(src, seg, n):
    return jax.ops.segment_sum(src, seg, n)
kernel_name = 'mk_audio_tower_d1_tok_audfeat512_r4_7a560d'

def setup_inputs(seed: int=0):
    np.random.seed(seed)
    _w = jnp.asarray

    def _rec_inputs():
        import jax
        import jax.numpy as jnp
        _rk = jax.random.key(seed)
        x = -0.000124254 + 0.999853 * jax.random.normal(jax.random.fold_in(_rk, 1), (8, 750, 128), jnp.float32)
        return x
    x = _rec_inputs()

    def _L0_tok_setup():
        import jax, jax.numpy as jnp
        import numpy as np
        CONTEXT = (-2, -1, 0, 1, 2)
        EPS = 1e-05
        key = jax.random.key(seed)
        k1, k2 = jax.random.split(key, 2)
        B, T, F = (64, 250, 128)
        O = 128
        C = len(CONTEXT)
        x = jax.random.normal(k1, (B, T, F), dtype=jnp.float32)
        W = jax.random.normal(k2, (O, F * C), dtype=jnp.float32) * 0.02
        b = jnp.zeros((O,), dtype=jnp.float32)
        gamma = jnp.ones((O,), dtype=jnp.float32)
        beta = jnp.zeros((O,), dtype=jnp.float32)
        return {'x': x, 'W': W, 'b': b, 'gamma': gamma, 'beta': beta}
    _L0_tok_all = _L0_tok_setup()
    _L0_tok_in = {k: v for k, v in _L0_tok_all.items() if k in ('W', 'b', 'gamma', 'beta')}
    del _L0_tok_all

    def _L0_attn_setup():
        import jax, jax.numpy as jnp
        import numpy as np
        EMBED_DIM = 128
        key = jax.random.key(seed)
        k1, k2, k3 = jax.random.split(key, 3)
        B, T, E = (8, 512, EMBED_DIM)
        x = jax.random.normal(k1, (B, T, E), dtype=jnp.float32)
        Wq = jax.random.normal(k2, (E, E), dtype=jnp.float32) * E ** (-0.5)
        bq = jnp.zeros((E,), dtype=jnp.float32)
        Wk = jax.random.normal(k3, (E, E), dtype=jnp.float32) * E ** (-0.5)
        bk = jnp.zeros((E,), dtype=jnp.float32)
        return {'x': x, 'Wq': Wq, 'bq': bq, 'Wk': Wk, 'bk': bk}
    _L0_attn_all = _L0_attn_setup()
    _L0_attn_in = {k: v for k, v in _L0_attn_all.items() if k in ('Wq', 'bq', 'Wk', 'bk')}
    del _L0_attn_all

    def _L0_ffn_setup():
        import jax, jax.numpy as jnp
        import numpy as np
        from jax import lax
        N, M, DIM, HEADS, TOPK = (4, 512, 128, 8, 16)

        def _split_heads(t, h):
            n, m, c = t.shape
            return t.reshape(n, m, h, c // h).transpose(0, 2, 1, 3).reshape(n * h, m, c // h)
        key = jax.random.key(seed)
        ks = jax.random.split(key, 7)
        f = lambda k, s, sc=1.0: jax.random.normal(k, s, dtype=jnp.float32) * sc
        return {'x': f(ks[0], (N, M, DIM)), 'pos_w': f(ks[1], (DIM, 1, 3), 0.1), 'pos_b': f(ks[2], (DIM,), 0.02), 'qkv_w': f(ks[3], (3 * DIM, DIM), 0.02), 'qkv_b': f(ks[4], (3 * DIM,), 0.02), 'wo_w': f(ks[5], (DIM, DIM), 0.02), 'wo_b': f(ks[6], (DIM,), 0.02)}
    _L0_ffn_all = _L0_ffn_setup()
    _L0_ffn_in = {k: v for k, v in _L0_ffn_all.items() if k in ('pos_w', 'pos_b', 'qkv_w', 'qkv_b', 'wo_w', 'wo_b')}
    del _L0_ffn_all
    return {'x': x, 'L0_tok_W': _L0_tok_in['W'], 'L0_tok_b': _L0_tok_in['b'], 'L0_tok_gamma': _L0_tok_in['gamma'], 'L0_tok_beta': _L0_tok_in['beta'], 'L0_attn_Wq': _L0_attn_in['Wq'], 'L0_attn_bq': _L0_attn_in['bq'], 'L0_attn_Wk': _L0_attn_in['Wk'], 'L0_attn_bk': _L0_attn_in['bk'], 'L0_ffn_pos_w': _L0_ffn_in['pos_w'], 'L0_ffn_pos_b': _L0_ffn_in['pos_b'], 'L0_ffn_qkv_w': _L0_ffn_in['qkv_w'], 'L0_ffn_qkv_b': _L0_ffn_in['qkv_b'], 'L0_ffn_wo_w': _L0_ffn_in['wo_w'], 'L0_ffn_wo_b': _L0_ffn_in['wo_b']}

def reference(x, L0_tok_W, L0_tok_b, L0_tok_gamma, L0_tok_beta, L0_attn_Wq, L0_attn_bq, L0_attn_Wk, L0_attn_bk, L0_ffn_pos_w, L0_ffn_pos_b, L0_ffn_qkv_w, L0_ffn_qkv_b, L0_ffn_wo_w, L0_ffn_wo_b):
    import jax
    import jax.numpy as jnp

    def _L0_tok_ref(x, W, b, gamma, beta):
        import jax, jax.numpy as jnp
        import numpy as np
        CONTEXT = (-2, -1, 0, 1, 2)
        EPS = 1e-05
        T = x.shape[1]
        width = CONTEXT[-1] - CONTEXT[0]
        T_out = T - width
        xc = jnp.concatenate([x[:, i:i + T_out, :] for i in range(len(CONTEXT))], axis=-1)
        h = jax.nn.relu(jnp.einsum('btf,of->bto', xc, W) + b)
        mean = jnp.mean(h, axis=(0, 1))
        var = jnp.mean(jnp.square(h - mean), axis=(0, 1))
        return gamma * (h - mean) * jax.lax.rsqrt(var + EPS) + beta

    def _L0_attn_ref(x, Wq, bq, Wk, bk):
        import jax, jax.numpy as jnp
        import numpy as np
        EMBED_DIM = 128
        scaling = jnp.float32(EMBED_DIM ** (-0.5))
        q = (x @ Wq + bq) * scaling
        k = x @ Wk + bk
        scores = jnp.einsum('bqe,bke->bqk', q, k)
        attn = jax.nn.softmax(scores, axis=-1)
        return jnp.einsum('bqk,bke->bqe', attn, x)

    def _L0_ffn_ref(x, pos_w, pos_b, qkv_w, qkv_b, wo_w, wo_b):
        import jax, jax.numpy as jnp
        import numpy as np
        from jax import lax
        N, M, DIM, HEADS, TOPK = (4, 512, 128, 8, 16)

        def _split_heads(t, h):
            n, m, c = t.shape
            return t.reshape(n, m, h, c // h).transpose(0, 2, 1, 3).reshape(n * h, m, c // h)
        n, m, c = x.shape
        h = HEADS
        scale = c ** (-0.5)
        pos = lax.conv_general_dilated(x.transpose(0, 2, 1), pos_w, window_strides=(1,), padding=[(1, 1)], feature_group_count=c, dimension_numbers=('NCH', 'OIH', 'NCH'))
        x = x + (pos + pos_b[None, :, None]).transpose(0, 2, 1)
        qkv = x @ qkv_w.T + qkv_b
        q, k, v = jnp.split(qkv, [c, 2 * c], axis=-1)
        q = _split_heads(q, h)
        k = _split_heads(k, h)
        v = _split_heads(v, h)
        qd = lax.stop_gradient(q)
        kd = lax.stop_gradient(k)
        logits = jnp.einsum('bmd,bpd->bmp', qd * scale, kd)
        _, idx = lax.top_k(logits, TOPK)
        gather = jax.vmap(lambda t, i: t[i])
        k_sel = gather(k, idx)
        v_sel = gather(v, idx)
        attn = jax.nn.softmax(jnp.einsum('bmd,bmkd->bmk', q * scale, k_sel), axis=-1)
        out = jnp.einsum('bmk,bmkd->bmd', attn, v_sel)
        d = c // h
        out = out.reshape(n, h, m, d).transpose(0, 2, 1, 3).reshape(n, m, c)
        return out @ wo_w.T + wo_b
    h = _L0_tok_ref(x, L0_tok_W, L0_tok_b, L0_tok_gamma, L0_tok_beta)
    h = h + _L0_attn_ref(_layernorm(h, axis=-1), L0_attn_Wq, L0_attn_bq, L0_attn_Wk, L0_attn_bk)
    h = h + _L0_ffn_ref(_layernorm(h, axis=-1), L0_ffn_pos_w, L0_ffn_pos_b, L0_ffn_qkv_w, L0_ffn_qkv_b, L0_ffn_wo_w, L0_ffn_wo_b)
    return h

_drawn_inputs = setup_inputs


def setup_inputs(seed=0):
    import zlib

    import numpy as np

    out = dict(_drawn_inputs(seed))
    spreads = {'L0_tok_b': (0.0, 0.1),
     'L0_tok_gamma': (1.0, 0.2),
     'L0_tok_beta': (0.0, 0.1),
     'L0_attn_bq': (0.0, 0.8),
     'L0_attn_bk': (0.0, 0.8)}
    factors = {'L0_ffn_pos_w': 7.004,
     'L0_ffn_pos_b': 8.0,
     'L0_ffn_qkv_w': 3.038,
     'L0_ffn_qkv_b': 8.0,
     'L0_ffn_wo_w': 3.015,
     'L0_ffn_wo_b': 2.868}
    for name, (base, spread) in spreads.items():
        noise = np.random.default_rng([zlib.crc32(name.encode()), seed]).standard_normal(out[name].shape)
        drawn = base * np.exp(spread * noise) if base else spread * noise
        out[name] = jnp.asarray(drawn.astype(out[name].dtype))
    for name, factor in factors.items():
        out[name] = (out[name] * factor).astype(out[name].dtype)
    return out
```

```python
from contextlib import ExitStack

import concourse.bass as bass
from concourse import mybir

P = 128
F32 = mybir.dt.float32
BF16 = mybir.dt.bfloat16
ALU = mybir.AluOpType
ACT = mybir.ActivationFunctionType
AX = mybir.AxisListType

FRONT = (["h_rows", "xn_cols", "q", "k", "S0", "S1"]
         + [n for t in range(4) for n in (f"PT{t}", f"S{t + 2}", f"PV{t}")]
         + ["PT4", "PV4", "PT5", "PV5", "y_cols", "q2", "k2", "v", "o_cols", "out"])
assert len(FRONT) % 4 == 0


def audio_tower_kernel(nc: bass.Bass, x, tok_W, tok_b, tok_gamma, tok_beta, attn_Wq, attn_bq, attn_Wk, attn_bk,
                       pos_w, pos_b, qkv_w, qkv_b, wo_w, wo_b, out):
    B, T, C = x.shape
    TAPS = tok_W.shape[1] // C
    N = T - TAPS + 1
    H2 = N // 2
    NT = -(-N // P)
    NP = NT * P
    LAST = N - (NT - 1) * P
    XR = T // NT
    HEADS = 8
    D = C // HEADS
    DA = D + 1
    SCALE = float(C) ** -0.5
    EPS = 1e-5
    WEIGHT_LOADS = 18
    TPB = HEADS * NT
    BODY = 2 * NT
    LAG = 3
    BIG = float(2.0 ** 80)
    KILL = float(2.0 ** 100)
    assert N == 2 * H2 and XR * NT == T and C == P and H2 <= 512 and NT == 6 and B % 2 == 0

    slot_of = {n: i % 4 for i, n in enumerate(FRONT)}
    use_of = {n: i // 4 for i, n in enumerate(FRONT)}
    USES = len(FRONT) // 4

    with ExitStack() as ctx:
        def sb(name, shape, dt=F32):
            return ctx.enter_context(nc.sbuf_tensor(name, shape, dt))

        def sem(name):
            return ctx.enter_context(nc.semaphore(name))

        pair = [ctx.enter_context(nc.psum_tensor(f"pair{i}", [P, 2, 512], F32)) for i in range(4)]

        ident = sb("ident", [P, P])
        neg_ident = sb("neg_ident", [P, P], BF16)
        ones_bf = sb("ones_bf", [P, P], BF16)
        W_rows = sb("W_rows", [P, TAPS, P])
        W_cols = sb("W_cols", [P, TAPS, P])
        Wq_sb = sb("Wq_sb", [P, P])
        Wk_sb = sb("Wk_sb", [P, P])
        qkv_rows = sb("qkv_rows", [P, 3, P])
        qkv_cols = sb("qkv_cols", [P, 3, P])
        wo_rows = sb("wo_rows", [P, P])
        wo_cols = sb("wo_cols", [P, P])
        vec = sb("vec", [P, 6])
        qkvb = sb("qkvb", [P, 2, 1])
        posw = sb("posw", [P, 3])
        vb_row = sb("vb_row", [P, 3, C])
        wob_row = sb("wob_row", [P, C])
        bq_s = sb("bq_s", [P, 1])
        q2b_s = sb("q2b_s", [P, 1])
        posw1 = sb("posw1", [P, 1])
        real = sb("real", [P, NT])
        neg_half = sb("neg_half", [P, NT])

        x_sb = sb("x_sb", [P, 2, NT, P])
        xT = sb("xT", [P, 2, T])
        hT = sb("hT", [P, B, N])
        stats = sb("stats", [P, B, 2, 6])
        tok_mv = sb("tok_mv", [P, 2])
        tok_ve = sb("tok_ve", [P, 1])
        tok_rstd = sb("tok_rstd", [P, 1])
        bn_scale = sb("bn_scale", [P, 1])
        bn_tmp = sb("bn_tmp", [P, 1])
        bn_bias = sb("bn_bias", [P, 1])

        hb = sb("hb", [P, NP])
        h1 = sb("h1", [P, NT, P])
        h2 = sb("h2", [P, NT, P])
        ln_stats = sb("ln_stats", [P, NT, 6])
        ln_mv = sb("ln_mv", [P, NT, 2])
        ln_ve = sb("ln_ve", [P, NT])
        ln_pow = sb("ln_pow", [P, NT])
        ln_rstd = sb("ln_rstd", [P, NT])
        xn = sb("xn", [P, NT, P])
        xnT = sb("xnT", [P, NP])
        qT = sb("qT", [P, NP])
        kT = sb("kT", [P, N])
        neg_max = sb("neg_max", [P, 2])
        prob = sb("prob", [P, 2, NP])
        row_sum = sb("row_sum", [P, 2])
        row_inv = sb("row_inv", [P, 2])
        probT = sb("probT", [P, 2, NT, P])
        yn = sb("yn", [P, NT, P])
        yT = sb("yT", [P, NP + 1])
        y2a = sb("y2a", [P, N])
        y2b = sb("y2b", [P, N])
        y2T = sb("y2T", [P, NP])
        qf = sb("qf", [P, 2, N])
        rem = sb("rem", [P, 2, N])
        parts = sb("parts", [P, 2, 3, NP], BF16)
        v_aug = sb("v_aug", [P, NT, HEADS, DA])

        stack = sb("stack", [P, 2, 2, NP], BF16)
        v_head = sb("v_head", [P, 2, NT, DA])
        top_a = sb("top_a", [P, 2, 8])
        top_b = sb("top_b", [P, 2, 8])
        rest = sb("rest", [P, 2, H2])
        thr = sb("thr", [P, 2])
        shift = sb("shift", [P, 2, P], BF16)
        pen = sb("pen", [P, 2, NP], BF16)
        wT = sb("wT", [P, 2, 2, 3 * P])
        o_raw = sb("o_raw", [P, NT, HEADS, DA])
        o_inv = sb("o_inv", [P, NT, HEADS])
        o_n = sb("o_n", [P, NT, HEADS, D])
        oT = sb("oT", [P, NP])
        h2b = sb("h2b", [P, NT, P])
        res = sb("res", [P, NT, P])

        s_w = sem("weights_loaded")
        s_xin = [sem(f"x_loaded{u}") for u in range(2)]
        s_mem = sem("memsets_done")
        s_id0 = sem("ident_zeroed")
        s_id = sem("ident_ready")
        s_wt = sem("weight_transposes")
        s_wc = sem("weight_copies")
        s_small = sem("small_constants")
        s_xps = sem("x_transposed")
        s_xT = sem("xT_in_sbuf")
        s_conv = sem("conv_products")
        s_h = sem("h_in_sbuf")
        s_bst = sem("batch_stats")
        s_bagg = sem("bn_chain")
        s_bpow = sem("bn_rstd")
        s_bn = sem("bn_affine_ready")
        s_full = [sem(f"pair{i}_full") for i in range(4)]
        s_drain = [sem(f"pair{i}_drained") for i in range(4)]
        s_hb = sem("h_normalised")
        s_lst = sem("ln_stats_done")
        s_lmv = sem("ln_mv_done")
        s_lve = sem("ln_var_eps")
        s_lpow = sem("ln_power")
        s_lrs = sem("ln_rstd_done")
        s_xn = sem("xn_ready")
        s_yn = sem("yn_ready")
        s_nmax = sem("attn_max")
        s_rinv = sem("attn_inverse")
        s_y2a = sem("pos_conv_step1")
        s_y2b = sem("pos_conv_step2")
        s_y2 = sem("y2T_ready")
        s_p1 = sem("qk_part1")
        s_rem = sem("qk_remainder")
        s_p2 = sem("qk_part2")
        s_p3 = sem("qk_part3")
        s_stack = [sem(f"stack{u}_loaded") for u in range(2)]
        s_vh = sem("v_head_ready")
        s_sc = sem("scores_ready")
        s_ta = sem("top_a_found")
        s_rest = sem("rest_ready")
        s_tb = sem("top_b_found")
        s_thr = sem("threshold_ready")
        s_shift = sem("shift_ready")
        s_pen = sem("penalty_ready")
        s_st = sem("masked_scoresT")
        s_wT = sem("weightsT_ready")
        s_pv = sem("head_output")
        s_o = sem("o_raw_ready")
        s_oinv = sem("o_inverse")
        s_on = sem("o_normalised")
        s_h2b = sem("h2_with_bias")
        s_out = sem("result_stored")

        def halves(ap):
            return ap.rearrange("p (h n) -> p h n", h=2)

        def full(eng, name, b):
            eng.wait_ge(s_full[slot_of[name]], b * USES + use_of[name] + 1)

        def copied(eng, name, b):
            eng.wait_ge(s_drain[slot_of[name]], b * USES + use_of[name] + 2)

        def apart(ins):
            return ins.wait_op(s_id0, 2, "sem-ge")

        block = ctx.enter_context(nc.Block())

        @block.sync
        def _(sp):
            for dst, src in (
                (W_rows[:], tok_W.rearrange("o (c f) -> o c f", c=TAPS)),
                (Wq_sb[:], attn_Wq), (Wk_sb[:], attn_Wk),
                (qkv_rows[:], qkv_w.rearrange("(j o) i -> o j i", j=3)),
                (wo_rows[:], wo_w),
                (posw[:], pos_w.rearrange("c a k -> c (a k)")),
                (vb_row[:, 0, :], qkv_b[2 * C:3 * C].partition_broadcast(P)),
                (vb_row[:, 1, :], qkv_b[2 * C:3 * C].partition_broadcast(P)),
                (vb_row[:, 2, :], qkv_b[2 * C:3 * C].partition_broadcast(P)),
                (wob_row[:], wo_b.partition_broadcast(P)),
            ):
                sp.dma_start(dst, src).then_inc(s_w, 16)
            for j in range(2):
                sp.dma_start(qkvb[:, j, :], qkv_b[C * j:C * (j + 1)].rearrange("(p a) -> p a", a=1)).then_inc(s_w, 16)
            for i, v in enumerate((tok_b, tok_gamma, tok_beta, attn_bq, attn_bk, pos_b)):
                sp.dma_start(vec[:, i:i + 1], v.rearrange("(p a) -> p a", a=1)).then_inc(s_w, 16)

            for u in range(2):
                sp.dma_start(x_sb[0:XR, u], x[u].rearrange("(t p) f -> p t f", p=XR)).then_inc(s_xin[u], 16)
            with sp.Fori(1, B // 2) as p:
                for u in range(2):
                    sp.wait_ge(s_xps, 2 * p + u - 1)
                    sp.dma_start(x_sb[0:XR, u], x[2 * p + u].rearrange("(t p) f -> p t f", p=XR)
                                 ).then_inc(s_xin[u], 16)

            sp.sem_inc(s_out, 16)
            with sp.Fori(0, B) as b:
                sp.wait_ge(s_p1, 2 * b + 2)
                sp.wait_ge(s_p2, 2 * b + 2)
                sp.wait_ge(s_p3, 2 * b + 2)
                for h in range(HEADS):
                    if h >= 2:
                        sp.wait_ge(s_st, b * TPB + NT * (h - 1))
                    u = h % 2
                    for i in range(3):
                        n = 3 if i < 2 else 2
                        for j in range(n):
                            g = 3 * i + j
                            sp.dma_start(stack[D * g:D * g + D, u, 0, :], parts[D * h:D * h + D, 0, i, :]
                                         ).then_inc(s_stack[u], 16)
                            sp.dma_start(stack[D * g:D * g + D, u, 1, :], parts[D * h:D * h + D, 1, j, :]
                                         ).then_inc(s_stack[u], 16)
                copied(sp, "out", b)
                sp.dma_start(out[b, 0:(NT - 1) * P, :].rearrange("(t p) c -> p t c", p=P), res[:, 0:NT - 1, :]
                             ).then_inc(s_out, 16)
                sp.dma_start(out[b, (NT - 1) * P:N, :], res[0:LAST, NT - 1, :]).then_inc(s_out, 16)
            sp.wait_ge(s_out, 32 * B + 16)

        @block.gpsimd
        def _(pool):
            nc.gpsimd.memset(ident[:], 0.0).then_inc(s_id0, 1)
            nc.gpsimd.memset(neg_ident[:], 0.0).then_inc(s_id0, 1)
            pool.wait_ge(s_id0, 2)
            nc.gpsimd.affine_select(out=ident[:], in_=ident[:], compare_op=ALU.not_equal, fill=1.0,
                                    base=0, pattern=[[-1, P]], channel_multiplier=1).then_inc(s_id, 1)
            nc.gpsimd.affine_select(out=neg_ident[:], in_=neg_ident[:], compare_op=ALU.not_equal, fill=-1.0,
                                    base=0, pattern=[[-1, P]], channel_multiplier=1).then_inc(s_id, 1)
            nc.gpsimd.memset(ones_bf[:], 1.0).then_inc(s_mem, 1)
            nc.gpsimd.memset(real[:], 1.0).then_inc(s_mem, 1)
            nc.gpsimd.memset(neg_half[:], -0.5).then_inc(s_mem, 1)
            nc.gpsimd.memset(hb[:, N:NP], 0.0).then_inc(s_mem, 1)
            nc.gpsimd.memset(qT[:, N:NP], 0.0).then_inc(s_mem, 1)
            nc.gpsimd.memset(prob[:, :, N:NP], 0.0).then_inc(s_mem, 1)
            nc.gpsimd.memset(yT[:, 0:1], 0.0).then_inc(s_mem, 1)
            nc.gpsimd.memset(y2T[:, N:NP], 0.0).then_inc(s_mem, 1)
            nc.gpsimd.memset(parts[:, :, :, N:NP], 0.0).then_inc(s_mem, 1)
            nc.gpsimd.memset(pen[:, :, N:NP], KILL).then_inc(s_mem, 1)
            nc.gpsimd.memset(v_aug[:, :, :, D:DA], 1.0).then_inc(s_mem, 1)
            pool.wait_ge(s_mem, 11)
            nc.gpsimd.affine_select(out=real[:], in_=real[:], compare_op=ALU.is_ge, fill=0.0, base=N - 1,
                                    pattern=[[-P, NT]], channel_multiplier=-1).then_inc(s_mem, 1)
            pool.wait_ge(s_w, 16 * WEIGHT_LOADS)
            nc.gpsimd.tensor_scalar(bq_s[:], vec[:, 3:4], SCALE, None, ALU.mult).then_inc(s_small, 1)
            nc.gpsimd.tensor_scalar(q2b_s[:], qkvb[:, 0, :], SCALE, None, ALU.mult).then_inc(s_small, 1)
            nc.gpsimd.tensor_scalar(posw1[:], posw[:, 1:2], 1.0, None, ALU.add).then_inc(s_small, 1)
            pool.wait_ge(s_bagg, 2)
            nc.gpsimd.tensor_tensor(tok_rstd[:], tok_ve[:], neg_half[:, 0:1], ALU.pow).then_inc(s_bpow, 1)

            with pool.Fori(0, B) as b:
                for ln in range(2):
                    pool.wait_ge(s_lmv, 2 * NT * b + NT * (ln + 1))
                    apart(nc.gpsimd.tensor_scalar(ln_ve[:], ln_mv[:, :, 1], EPS, None, ALU.add)).then_inc(s_lve, 1)
                    pool.wait_ge(s_lve, 2 * b + ln + 1)
                    nc.gpsimd.tensor_tensor(ln_pow[:], ln_ve[:], neg_half[:], ALU.pow).then_inc(s_lpow, 1)
                    pool.wait_ge(s_mem, 12)
                    pool.wait_ge(s_lpow, 2 * b + ln + 1)
                    nc.gpsimd.tensor_tensor(ln_rstd[:], ln_pow[:], real[:], ALU.mult).then_inc(s_lrs, 1)
                for w in range(2):
                    copied(pool, ("q2", "k2")[w], b)
                    pool.wait_ge(s_p1, 2 * b + w + 1)
                    nc.gpsimd.tensor_tensor(rem[:, w, :], qf[:, w, :], parts[:, w, 0, 0:N], ALU.subtract
                                            ).then_inc(s_rem, 1)
                for w in range(2):
                    pool.wait_ge(s_rem, 2 * b + w + 1)
                    pool.wait_ge(s_p2, 2 * b + w + 1)
                    nc.gpsimd.tensor_tensor(parts[:, w, 2, 0:N], rem[:, w, :], parts[:, w, 1, 0:N], ALU.subtract
                                            ).then_inc(s_p3, 1)

                def step(p, k, first):
                    n = b * TPB + BODY * p + k
                    s = k % 2
                    if k % NT == 0:
                        if first and k == 0:
                            copied(pool, "v", b)
                        if not (first and k < BODY):
                            pool.wait_ge(s_pv, n - NT)
                        u = (k // NT) % 2
                        apart(nc.gpsimd.tensor_copy(v_head[:, u, :, :], v_aug[:, :, 2 * p + k // NT, :])).then_inc(s_vh, 1)
                    pool.wait_ge(s_tb, n + 1)
                    if not (first and k < 2):
                        pool.wait_ge(s_pen, n - 1)
                    apart(nc.gpsimd.tensor_scalar(thr[:, s:s + 1], top_b[:, s, 7:8], BIG, None, ALU.mult
                                            )).then_inc(s_thr, 1)
                    if not (first and k < 2):
                        pool.wait_ge(s_st, n - 1)
                    apart(nc.gpsimd.tensor_scalar(shift[:, s, :], neg_ident[:], top_a[:, s, 0:1], None, ALU.mult
                                            )).then_inc(s_shift, 1)

                for k in range(BODY):
                    step(0, k, True)
                with pool.Fori(1, TPB // BODY) as p:
                    for k in range(BODY):
                        step(p, k, False)
                copied(pool, f"PV{NT - 1}", b)
                for t in range(NT):
                    nc.gpsimd.tensor_tensor(h2b[:, t, :], h2[:, t, :], wob_row[:], ALU.add).then_inc(s_h2b, 1)

        @block.tensor
        def _(pe):
            def mm(o, l, r, start=True, stop=True):
                return nc.tensor.matmul(o, lhsT=l, rhs=r, start=start, stop=stop, skip_group_check=True)

            pe.wait_ge(s_w, 16 * WEIGHT_LOADS)
            pe.wait_ge(s_id, 2)
            for c in range(TAPS):
                last = nc.tensor.transpose(pair[0][:, c // 3, P * (c % 3):P * (c % 3 + 1)], W_rows[:, c, :], ident[:])
            last.then_inc(s_wt, 1)
            for j in range(3):
                nc.tensor.transpose(pair[1][:, 0, P * j:P * (j + 1)], qkv_rows[:, j, :], ident[:])
            nc.tensor.transpose(pair[1][:, 1, 0:P], wo_rows[:], ident[:]).then_inc(s_wt, 1)
            pe.wait_ge(s_wc, 4)

            def tok(p, first):
                for u in range(2):
                    pe.wait_ge(s_xin[u], 16 * (p + 1))
                    if not first:
                        pe.wait_ge(s_xT, 2 * p + u - 1)
                    for t in range(NT):
                        last = nc.tensor.transpose(pair[u][:, t // 3, XR * (t % 3):XR * (t % 3 + 1)],
                                                   x_sb[0:XR, u, t, :], ident[0:XR, 0:XR])
                    last.then_inc(s_xps, 1)
                for u in range(2):
                    pe.wait_ge(s_xT, 2 * p + u + 1)
                    if not first:
                        pe.wait_ge(s_h, 2 * p + u - 1)
                    for f in range(2):
                        for c in range(TAPS):
                            last = mm(pair[2 + u][:, f, 0:H2], W_cols[:, c, :], xT[:, u, H2 * f + c:H2 * f + c + H2],
                                      c == 0, c == TAPS - 1)
                    last.then_inc(s_conv, 1)

            tok(0, True)
            with pe.Fori(1, B // 2) as p:
                tok(p, False)
            pe.wait_ge(s_xT, B)
            pe.wait_ge(s_h, B)
            for s in range(4):
                pe.sem_inc(s_drain[s], 1)

            def batch(b):
                def begin(name):
                    pe.wait_ge(s_drain[slot_of[name]], b * USES + use_of[name] + 1)
                    return pair[slot_of[name]], s_full[slot_of[name]]

                def source(name, job):
                    if slot_of[name] != slot_of[job]:
                        copied(pe, name, b)

                def turn(name, src):
                    o, full_sem = begin(name)
                    for t in range(NT):
                        last = nc.tensor.transpose(o[:, t // 3, P * (t % 3):P * (t % 3 + 1)], src(t), ident[:])
                    last.then_inc(full_sem, 1)

                def project(name, w, src):
                    o, full_sem = begin(name)
                    for f in range(2):
                        last = mm(o[:, f, 0:H2], w, src[:, H2 * f:H2 * (f + 1)])
                    last.then_inc(full_sem, 1)

                def score(t):
                    o, full_sem = begin(f"S{t}")
                    for f in range(2):
                        last = mm(o[:, f, 0:H2], qT[:, P * t:P * (t + 1)], kT[:, H2 * f:H2 * (f + 1)])
                    last.then_inc(full_sem, 1)

                def turn_probs(t):
                    source(f"S{t}", f"PT{t}")
                    turn(f"PT{t}", lambda j: prob[:, t % 2, P * j:P * (j + 1)])

                def mix(t):
                    source(f"PT{t}", f"PV{t}")
                    o, full_sem = begin(f"PV{t}")
                    for j in range(NT):
                        last = mm(o[:, 0, 0:P], probT[:, t % 2, j, :], xn[:, j, :], j == 0, j == NT - 1)
                    last.then_inc(full_sem, 1)

                pe.wait_ge(s_hb, b + 1)
                turn("h_rows", lambda t: hb[:, P * t:P * (t + 1)])
                pe.wait_ge(s_xn, b + 1)
                turn("xn_cols", lambda t: xn[:, t, :])
                source("xn_cols", "q")
                project("q", Wq_sb[:], xnT)
                project("k", Wk_sb[:], xnT)
                source("q", "S0")
                source("k", "S0")
                score(0)
                score(1)
                for t in range(NT):
                    turn_probs(t)
                    if t + 2 < NT:
                        score(t + 2)
                    mix(t)
                pe.wait_ge(s_yn, b + 1)
                turn("y_cols", lambda t: yn[:, t, :])
                pe.wait_ge(s_y2, b + 1)
                project("q2", qkv_cols[:, 0, :], y2T)
                project("k2", qkv_cols[:, 1, :], y2T)
                o, full_sem = begin("v")
                for t in range(NT):
                    last = mm(o[:, t // 3, P * (t % 3):P * (t % 3 + 1)], y2T[:, P * t:P * (t + 1)], qkv_cols[:, 2, :])
                last.then_inc(full_sem, 1)
                for s in range(4):
                    pe.wait_ge(s_drain[s], b * USES + 1 + sum(slot_of[n] == s for n in FRONT[:-2]))

                def step(p, k, head, tail):
                    n = b * TPB + BODY * p + k
                    s = k % 2
                    if not tail or k < BODY:
                        u = (k // NT) % 2
                        if k % NT == 0:
                            pe.wait_ge(s_stack[u], 256 * (b * (HEADS // 2) + p + k // BODY + 1))
                        if not head or k >= 2:
                            pe.wait_ge(s_pen, n - 1)
                        for f in range(2):
                            last = mm(pair[s][:, f, 0:H2], stack[:, u, 0, P * (k % NT):P * (k % NT + 1)],
                                      stack[:, u, 1, H2 * f:H2 * (f + 1)])
                        last.then_inc(s_sc, 1)
                    if (not head or k >= 2) and (not tail or k - 2 < BODY):
                        kk, m = k - 2, n - 2
                        u = (kk // NT) % 2
                        pe.wait_ge(s_shift, m + 1)
                        pe.wait_ge(s_pen, m + 1)
                        if not head or kk >= 2:
                            pe.wait_ge(s_wT, m - 1)
                            pe.wait_ge(s_o, m - 1)
                        o = pair[2 + s]
                        for f in range(2):
                            mm(o[:, f, 0:3 * P].rearrange("p (j q) -> p j q", j=3), ones_bf[:],
                               shift[:, s:s + 1, :].broadcast_to([P, 3, P]), True, False)
                            for j in range(3):
                                col = P * (3 * f + j)
                                dst = o[:, f, P * j:P * (j + 1)]
                                mm(dst, stack[:, u, 1, col:col + P], stack[:, u, 0, P * (kk % NT):P * (kk % NT + 1)],
                                   False, False)
                                last = mm(dst, pen[:, s, col:col + P], neg_ident[:], False, j == 2)
                        last.then_inc(s_st, 1)
                    if not head or k >= 3:
                        kk, m = k - 3, n - 3
                        u = (kk // NT) % 2
                        if kk % NT == 0:
                            pe.wait_ge(s_vh, b * HEADS + 2 * p + kk // NT + 1)
                        pe.wait_ge(s_wT, m + 1)
                        for j in range(NT):
                            last = mm(pair[3 - s][:, 1, 3 * P:3 * P + DA],
                                      wT[:, 1 - s, j // 3, P * (j % 3):P * (j % 3 + 1)], v_head[:, u, j, :],
                                      j == 0, j == NT - 1)
                        last.then_inc(s_pv, 1)

                for k in range(LAG):
                    step(0, k, True, False)
                for k in range(LAG, BODY + LAG):
                    step(0, k, True, False)
                with pe.Fori(1, TPB // BODY - 1) as p:
                    for k in range(LAG, BODY + LAG):
                        step(p, k, False, False)
                for k in range(LAG, BODY + LAG):
                    step(TPB // BODY - 1, k, False, True)

                pe.wait_ge(s_on, b + 1)
                turn("o_cols", lambda t: o_n[:, t, :, :].rearrange("p h d -> p (h d)"))
                source("o_cols", "out")
                o, full_sem = begin("out")
                for t in range(NT):
                    last = mm(o[:, t // 3, P * (t % 3):P * (t % 3 + 1)], oT[:, P * t:P * (t + 1)], wo_cols[:])
                last.then_inc(full_sem, 1)

            with pe.Fori(0, B) as b:
                batch(b)

        @block.scalar
        def _(act):
            act.wait_ge(s_wt, 2)
            nc.scalar.activation(W_cols[:, 0:3, :], pair[0][:, 0, 0:3 * P], ACT.Copy).then_inc(s_wc, 1)
            nc.scalar.activation(W_cols[:, 3:TAPS, :], pair[0][:, 1, 0:(TAPS - 3) * P], ACT.Copy).then_inc(s_wc, 1)
            nc.scalar.activation(qkv_cols[:], pair[1][:, 0, 0:3 * P], ACT.Copy).then_inc(s_wc, 1)
            nc.scalar.activation(wo_cols[:], pair[1][:, 1, 0:P], ACT.Copy).then_inc(s_wc, 1)

            def tok(p, first):
                for u in range(2):
                    act.wait_ge(s_xps, 2 * p + u + 1)
                    if not first:
                        act.wait_ge(s_conv, 2 * p + u - 1)
                    nc.scalar.activation(halves(xT[:, u, :]), pair[u][:, :, 0:T // 2], ACT.Copy).then_inc(s_xT, 1)
                for u in range(2):
                    act.wait_ge(s_conv, 2 * p + u + 1)
                    nc.scalar.activation(halves(hT[:, 2 * p + u, :]), pair[2 + u][:, :, 0:H2], ACT.Relu,
                                         bias=vec[:, 0:1]).then_inc(s_h, 1)

            tok(0, True)
            with act.Fori(1, B // 2) as p:
                tok(p, False)
            act.wait_ge(s_bn, 1)
            act.wait_ge(s_small, 3)
            act.wait_ge(s_mem, 11)

            def batch(b):
                def drained(ins, name):
                    ins.then_inc(s_drain[slot_of[name]], 1)

                def rows(name):
                    return pair[slot_of[name]][:, :, 0:3 * P]

                def cols(name):
                    return pair[slot_of[name]][:, :, 0:H2]

                nc.scalar.activation(hb[:, 0:N], hT[:, b, :], ACT.Identity, bias=bn_bias[:], scale=bn_scale[:]
                                     ).then_inc(s_hb, 1)
                full(act, "h_rows", b)
                drained(nc.scalar.activation(h1[:].rearrange("p (f t) c -> p f (t c)", f=2), rows("h_rows"),
                                             ACT.Copy), "h_rows")
                full(act, "xn_cols", b)
                drained(nc.scalar.activation(halves(xnT[:]), rows("xn_cols"), ACT.Copy), "xn_cols")
                full(act, "q", b)
                drained(nc.scalar.activation(halves(qT[:, 0:N]), cols("q"), ACT.Identity, bias=bq_s[:],
                                             scale=SCALE), "q")
                full(act, "k", b)
                drained(nc.scalar.activation(halves(kT[:]), cols("k"), ACT.Identity, bias=vec[:, 4:5]), "k")
                for t in range(NT):
                    act.wait_ge(s_nmax, NT * b + t + 1)
                    if t >= 2:
                        full(act, f"PT{t - 2}", b)
                        act.wait_ge(s_rinv, NT * b + t - 1)
                    drained(nc.scalar.activation(halves(prob[:, t % 2, 0:N]), cols(f"S{t}"), ACT.Exp,
                                                 bias=neg_max[:, t % 2:t % 2 + 1],
                                                 accum_out=row_sum[:, t % 2:t % 2 + 1]), f"S{t}")
                full(act, "y_cols", b)
                drained(nc.scalar.activation(halves(yT[:, 1:NP + 1]), rows("y_cols"), ACT.Copy), "y_cols")
                full(act, "q2", b)
                drained(nc.scalar.activation(halves(qf[:, 0, :]), cols("q2"), ACT.Identity, bias=q2b_s[:],
                                             scale=SCALE), "q2")
                full(act, "k2", b)
                drained(nc.scalar.activation(halves(qf[:, 1, :]), cols("k2"), ACT.Identity, bias=qkvb[:, 1, :]), "k2")

                def step(p, k, head, tail):
                    n = b * TPB + BODY * p + k
                    s = k % 2
                    if not tail or k < BODY:
                        act.wait_ge(s_thr, n + 1)
                        if not head or k >= 2:
                            act.wait_ge(s_st, n - 1)
                        nc.scalar.activation(halves(pen[:, s, 0:N]), pair[s][:, :, 0:H2], ACT.Relu,
                                             bias=thr[:, s:s + 1], scale=-BIG).then_inc(s_pen, 1)
                    if (not head or k >= 1) and (not tail or k - 1 < BODY):
                        m = n - 1
                        act.wait_ge(s_st, m + 1)
                        if not head or k - 1 >= 2:
                            act.wait_ge(s_pv, m - 1)
                        nc.scalar.activation(wT[:, 1 - s], pair[3 - s][:, :, 0:3 * P], ACT.Exp).then_inc(s_wT, 1)
                    if (not head or k >= 2) and (not tail or k - 2 < BODY):
                        kk, m = k - 2, n - 2
                        act.wait_ge(s_pv, m + 1)
                        nc.scalar.activation(o_raw[:, kk % NT, 2 * p + kk // NT, :],
                                             pair[2 + s][:, 1, 3 * P:3 * P + DA], ACT.Copy).then_inc(s_o, 1)

                for k in range(BODY + LAG):
                    step(0, k, True, False)
                with act.Fori(1, TPB // BODY - 1) as p:
                    for k in range(LAG, BODY + LAG):
                        step(p, k, False, False)
                for k in range(LAG, BODY + LAG):
                    step(TPB // BODY - 1, k, False, True)
                full(act, "o_cols", b)
                drained(nc.scalar.activation(halves(oT[:]), rows("o_cols"), ACT.Copy), "o_cols")

            with act.Fori(0, B) as b:
                batch(b)

        @block.vector
        def _(dve):
            with dve.Fori(0, B // 2) as p:
                for u in range(2):
                    dve.wait_ge(s_h, 2 * p + u + 1)
                    for f in range(2):
                        nc.vector.bn_stats(stats[:, 2 * p + u, f, :], hT[:, 2 * p + u, H2 * f:H2 * (f + 1)]
                                           ).then_inc(s_bst, 1)
            dve.wait_ge(s_bst, 2 * B)
            nc.vector.bn_aggr(tok_mv[:], stats[:].rearrange("p b f s -> p (b f s)")).then_inc(s_bagg, 1)
            dve.wait_ge(s_bagg, 1)
            nc.vector.tensor_scalar(tok_ve[:], tok_mv[:, 1:2], EPS, None, ALU.add).then_inc(s_bagg, 1)
            dve.wait_ge(s_bpow, 1)
            dve.wait_ge(s_w, 16 * WEIGHT_LOADS)
            nc.vector.tensor_tensor(bn_scale[:], tok_rstd[:], vec[:, 1:2], ALU.mult).then_inc(s_bagg, 1)
            dve.wait_ge(s_bagg, 3)
            nc.vector.tensor_tensor(bn_tmp[:], tok_mv[:, 0:1], bn_scale[:], ALU.mult).then_inc(s_bagg, 1)
            dve.wait_ge(s_bagg, 4)
            nc.vector.tensor_tensor(bn_bias[:], vec[:, 2:3], bn_tmp[:], ALU.subtract).then_inc(s_bn, 1)
            dve.wait_ge(s_small, 3)

            with dve.Fori(0, B) as b:
                def drained(ins, name):
                    ins.then_inc(s_drain[slot_of[name]], 1)

                def layernorm(src, dst, ln, done):
                    for t in range(NT):
                        nc.vector.bn_stats(ln_stats[:, t, :], src[:, t, :]).then_inc(s_lst, 1)
                    for t in range(NT):
                        dve.wait_ge(s_lst, (2 * b + ln) * NT + t + 1)
                        apart(nc.vector.bn_aggr(ln_mv[:, t, :], ln_stats[:, t, :])).then_inc(s_lmv, 1)
                    dve.wait_ge(s_lmv, (2 * b + ln + 1) * NT)
                    dve.wait_ge(s_lrs, 2 * b + ln + 1)
                    for t in range(NT):
                        last = nc.vector.tensor_scalar(dst[:, t, :], src[:, t, :], ln_mv[:, t, 0:1],
                                                       ln_rstd[:, t:t + 1], ALU.subtract, ALU.mult)
                    last.then_inc(done, 1)

                copied(dve, "h_rows", b)
                layernorm(h1, xn, 0, s_xn)

                def attn_max(t):
                    full(dve, f"S{t}", b)
                    if t >= 2:
                        copied(dve, f"S{t - 2}", b)
                    nc.vector.tensor_reduce(neg_max[:, t % 2:t % 2 + 1], pair[slot_of[f"S{t}"]][:, :, 0:H2],
                                            AX.XY, ALU.max, negate=True).then_inc(s_nmax, 1)

                attn_max(0)
                for t in range(NT):
                    if t + 1 < NT:
                        attn_max(t + 1)
                    full(dve, f"PT{t}", b)
                    if t >= 2:
                        full(dve, f"PV{t - 2}", b)
                    drained(nc.vector.tensor_copy(probT[:, t % 2].rearrange("p (f j) q -> p f (j q)", f=2),
                                                  pair[slot_of[f"PT{t}"]][:, :, 0:3 * P]), f"PT{t}")
                    copied(dve, f"S{t}", b)
                    nc.vector.reciprocal(row_inv[:, t % 2:t % 2 + 1], row_sum[:, t % 2:t % 2 + 1]).then_inc(s_rinv, 1)
                    full(dve, f"PV{t}", b)
                    dve.wait_ge(s_rinv, NT * b + t + 1)
                    drained(nc.vector.scalar_tensor_tensor(h2[:, t, :], pair[slot_of[f"PV{t}"]][:, 0, 0:P],
                                                           row_inv[:, t % 2:t % 2 + 1], h1[:, t, :],
                                                           ALU.mult, ALU.add), f"PV{t}")
                for name in {slot_of[f"PV{t}"]: f"PV{t}" for t in range(NT)}.values():
                    copied(dve, name, b)
                layernorm(h2, yn, 1, s_yn)

                copied(dve, "y_cols", b)
                nc.vector.tensor_scalar(y2a[:], yT[:, 1:N + 1], posw1[:], vec[:, 5:6], ALU.mult, ALU.add
                                        ).then_inc(s_y2a, 1)
                dve.wait_ge(s_y2a, b + 1)
                nc.vector.scalar_tensor_tensor(y2b[:], yT[:, 0:N], posw[:, 0:1], y2a[:], ALU.mult, ALU.add
                                               ).then_inc(s_y2b, 1)
                dve.wait_ge(s_y2b, b + 1)
                nc.vector.scalar_tensor_tensor(y2T[:, 0:N], yT[:, 2:N + 2], posw[:, 2:3], y2b[:], ALU.mult, ALU.add
                                               ).then_inc(s_y2, 1)

                for w in range(2):
                    copied(dve, ("q2", "k2")[w], b)
                    nc.vector.tensor_copy(parts[:, w, 0, 0:N], qf[:, w, :]).then_inc(s_p1, 1)
                full(dve, "v", b)
                drained(nc.vector.tensor_tensor(
                    v_aug[:].rearrange("p (f t) h d -> p f (t h) d", f=2)[:, :, :, 0:D],
                    pair[slot_of["v"]][:, :, 0:3 * P].rearrange("p f (g d) -> p f g d", d=D),
                    vb_row[:].rearrange("p t (h d) -> p (t h) d", d=D).unsqueeze(1).broadcast_to([P, 2, 3 * HEADS, D]),
                    ALU.add), "v")
                for w in range(2):
                    dve.wait_ge(s_rem, 2 * b + w + 1)
                    nc.vector.tensor_copy(parts[:, w, 1, 0:N], rem[:, w, :]).then_inc(s_p2, 1)

                def step(p, k, head):
                    n = b * TPB + BODY * p + k
                    s = k % 2
                    scores = pair[s][:, :, 0:H2]
                    dve.wait_ge(s_sc, n + 1)
                    if not head or k >= 2:
                        dve.wait_ge(s_shift, n - 1)
                        dve.wait_ge(s_thr, n - 1)
                    apart(nc.vector.max(top_a[:, s, :], scores)).then_inc(s_ta, 1)
                    dve.wait_ge(s_ta, n + 1)
                    apart(nc.vector.match_replace(rest[:], top_a[:, s, :], scores, -3.0e38)).then_inc(s_rest, 1)
                    dve.wait_ge(s_rest, n + 1)
                    apart(nc.vector.max(top_b[:, s, :], rest[:])).then_inc(s_tb, 1)

                for k in range(BODY):
                    step(0, k, True)
                with dve.Fori(1, TPB // BODY) as p:
                    for k in range(BODY):
                        step(p, k, False)

                dve.wait_ge(s_o, (b + 1) * TPB)
                nc.vector.reciprocal(o_inv[:], o_raw[:, :, :, D]).then_inc(s_oinv, 1)
                dve.wait_ge(s_oinv, b + 1)
                nc.vector.tensor_tensor(o_n[:].rearrange("p t h d -> p (t h) d"),
                                        o_raw[:].rearrange("p t h d -> p (t h) d")[:, :, 0:D],
                                        o_inv[:].rearrange("p t h -> p (t h)").unsqueeze(2).broadcast_to(
                                            [P, NT * HEADS, D]), ALU.mult).then_inc(s_on, 1)
                full(dve, "out", b)
                dve.wait_ge(s_h2b, NT * b + NT)
                dve.wait_ge(s_out, 32 * b + 16)
                drained(nc.vector.tensor_tensor(res[:].rearrange("p (f t) c -> p f (t c)", f=2),
                                                pair[slot_of["out"]][:, :, 0:3 * P],
                                                h2b[:].rearrange("p (f t) c -> p f (t c)", f=2), ALU.add), "out")


_INS = ['x', 'L0_tok_W', 'L0_tok_b', 'L0_tok_gamma', 'L0_tok_beta', 'L0_attn_Wq', 'L0_attn_bq', 'L0_attn_Wk',
        'L0_attn_bk', 'L0_ffn_pos_w', 'L0_ffn_pos_b', 'L0_ffn_qkv_w', 'L0_ffn_qkv_b', 'L0_ffn_wo_w', 'L0_ffn_wo_b']
_OUTS = [((8, 746, 128), 'float32')]


def kernel(**inputs):
    import numpy as _np
    import concourse.bacc as _bacc
    from concourse import mybir as _mybir
    from concourse.bass_utils import run_bass_kernel_spmd as _run

    nc = _bacc.Bacc("TRN2", target_bir_lowering=False, num_devices=1)
    arrays, args = {}, []
    for name in _INS:
        a = _np.ascontiguousarray(inputs[name])
        arrays[f"in_{name}_dram"] = a
        args.append(nc.dram_tensor(f"in_{name}_dram", a.shape, _mybir.dt.from_np(a.dtype), kind="ExternalInput").ap())
    for i, (shape, dtype) in enumerate(_OUTS):
        dt = _mybir.dt.from_np(_np.dtype(dtype))
        args.append(nc.dram_tensor(f"out_{i}_dram", shape, dt, kind="ExternalOutput").ap())
    audio_tower_kernel(nc, *args)
    r = _run(nc, [arrays], core_ids=[0])
    got = tuple(r.results[0][f"out_{i}_dram"] for i in range(len(_OUTS)))
    return got[0]
```

```python
from contextlib import ExitStack

import concourse.bass as bass
from concourse import mybir

P = 128
F32 = mybir.dt.float32
BF16 = mybir.dt.bfloat16
ALU = mybir.AluOpType
ACT = mybir.ActivationFunctionType
AX = mybir.AxisListType

FRONT = {(9, "F"): "h_rows0", (9, "G"): "h_rows1", (13, "F"): "xn_cols0", (13, "G"): "xn_cols1",
         (14, "F"): "q0", (14, "G"): "q1", (15, "F"): "k0", (15, "G"): "k1"}
for _t in range(6):
    FRONT |= {(16 + 3 * _t, "F"): f"S0.{_t}", (16 + 3 * _t, "G"): f"S1.{_t}",
              (18 + 3 * _t, "F"): f"P0.{_t}", (18 + 3 * _t, "G"): f"P1.{_t}", (20 + 3 * _t, "F"): f"A0.{_t}"}
FRONT |= {(39, "F"): "y_cols0", (39, "G"): "y_cols1", (41, "G"): "qh0", (42, "F"): "qh1", (42, "G"): "kh0",
          (43, "F"): "kh1", (43, "G"): "v0", (44, "F"): "v1"}
END = {(53, "F"): "o_cols0", (53, "G"): "o_cols1", (54, "F"): "out0", (54, "G"): "out1"}
FRONT_NO = {name: n for n, (_, name) in enumerate(sorted(FRONT.items()))}
END_NO = {name: n for n, (_, name) in enumerate(sorted(END.items()))}
FIRST, LAST_PERIOD = 8, 56


def audio_tower_kernel(nc: bass.Bass, x, tok_W, tok_b, tok_gamma, tok_beta, attn_Wq, attn_bq, attn_Wk, attn_bk,
                       pos_w, pos_b, qkv_w, qkv_b, wo_w, wo_b, out):
    B, T, C = x.shape
    TAPS = tok_W.shape[1] // C
    N = T - TAPS + 1
    H2 = N // 2
    NT = -(-N // P)
    NP = NT * P
    LAST = N - (NT - 1) * P
    XR = T // NT
    HEADS = 8
    D = C // HEADS
    DA = D + 1
    SCALE = float(C) ** -0.5
    EPS = 1e-5
    WEIGHT_LOADS = 16
    TPB = HEADS * NT
    BIG = float(2.0 ** 80)
    assert N == 2 * H2 and XR * NT == T and C == P and H2 <= 512 and NT == 6 and B % 2 == 0

    NF, NE = len(FRONT), len(END)

    def front_no(fb, name):
        n = FRONT_NO[name]
        return n if isinstance(fb, int) and fb == 0 else (NF + NE) * fb - NE + n

    def end_no(b, name):
        before = 0 if isinstance(b, int) and b == B - 1 else NF
        return (NF + NE) * (b + 1) - NE + before + END_NO[name]

    with ExitStack() as ctx:
        def sb(name, shape, dt=F32):
            return ctx.enter_context(nc.sbuf_tensor(name, shape, dt))

        def sem(name):
            return ctx.enter_context(nc.semaphore(name))

        pair = [ctx.enter_context(nc.psum_tensor(f"pair{i}", [P, 2, 512], F32)) for i in range(4)]

        ident = sb("ident", [P, P])
        neg_ident = sb("neg_ident", [P, P], BF16)
        neg_big = sb("neg_big", [P, P], BF16)
        ones_bf = sb("ones_bf", [P, P], BF16)
        W_rows = sb("W_rows", [P, TAPS, P])
        W_cols = sb("W_cols", [P, TAPS, P])
        Wq_sb = sb("Wq_sb", [P, P])
        Wk_sb = sb("Wk_sb", [P, P])
        qkv_rows = sb("qkv_rows", [P, 3, P])
        qkv_cols = sb("qkv_cols", [P, 3, P])
        wo_rows = sb("wo_rows", [P, P])
        wo_cols = sb("wo_cols", [P, P])
        vec = sb("vec", [P, 6])
        qkvb = sb("qkvb", [P, 2, 1])
        posw = sb("posw", [P, 3])
        vb_row = sb("vb_row", [P, C])
        wob_row = sb("wob_row", [P, C])
        bq_s = sb("bq_s", [P, 1])
        q2b_s = sb("q2b_s", [P, 1])
        posw1 = sb("posw1", [P, 1])
        real = sb("real", [P, NT])
        neg_half = sb("neg_half", [P, NT])

        x_sb = sb("x_sb", [P, 2, NT, P])
        xT = sb("xT", [P, 2, T])
        hT = sb("hT", [P, B, NP])
        stats = sb("stats", [P, B, 2, 6])
        tok_mv = sb("tok_mv", [P, 2])
        tok_ve = sb("tok_ve", [P, 1])
        tok_rstd = sb("tok_rstd", [P, 1])
        bn_scale = sb("bn_scale", [P, 1])
        bn_tmp = sb("bn_tmp", [P, 1])
        bn_bias = sb("bn_bias", [P, 1])

        hb = sb("hb", [P, NP])
        h1 = sb("h1", [P, NT, P])
        h2 = sb("h2", [P, NT, P])
        ln_stats = sb("ln_stats", [P, NT, 6])
        ln_mv = sb("ln_mv", [P, NT, 2])
        ln_ve = sb("ln_ve", [P, NT])
        ln_pow = sb("ln_pow", [P, NT])
        ln_rstd = sb("ln_rstd", [P, NT])
        xn = sb("xn", [P, NT, P])
        xnT = sb("xnT", [P, NP])
        qT = sb("qT", [P, NP])
        kT = sb("kT", [P, N])
        att_sc = sb("att_sc", [P, N])
        neg_max = sb("neg_max", [P, 1])
        prob = sb("prob", [P, NP])
        row_sum = sb("row_sum", [P, 1])
        row_inv = sb("row_inv", [P, 1])
        probT = sb("probT", [P, NT, P])
        att = sb("att", [P, P])
        yn = sb("yn", [P, NT, P])
        yT = sb("yT", [P, NP + 1])
        y2a = sb("y2a", [P, N])
        y2b = sb("y2b", [P, N])
        y2T = sb("y2T", [P, NP])
        qf = sb("qf", [P, 2, N])
        rem = sb("rem", [P, 2, N])
        parts = sb("parts", [P, 2, 3, NP], BF16)
        v_rows = sb("v_rows", [P, NT, P])
        v_aug = sb("v_aug", [P, NT, HEADS, DA])

        stack = sb("stack", [P, 2, 2, NP], BF16)
        v_head = sb("v_head", [P, 2, NT, DA])
        top_a = sb("top_a", [P, 2, 8])
        top_b = sb("top_b", [P, 2, 8])
        rest = sb("rest", [P, 2, H2])
        shift = sb("shift", [P, 2, P], BF16)
        pen = sb("pen", [P, 2, NP], BF16)
        wT = sb("wT", [P, 2, 2, 3 * P])
        o_raw = sb("o_raw", [P, B, NT, HEADS * DA])
        o_inv = sb("o_inv", [P, NT, HEADS])
        o_n = sb("o_n", [P, NT, HEADS, D])
        oT = sb("oT", [P, NP])
        proj = sb("proj", [P, NT, P])
        res = sb("res", [P, NT, P])

        s_w = sem("weights_loaded")
        s_xin = [sem(f"x_loaded{u}") for u in range(2)]
        s_mem = sem("memsets_done")
        s_id0 = sem("ident_zeroed")
        s_id = sem("ident_ready")
        s_wt = sem("weight_transposes")
        s_wc = sem("weight_copies")
        s_small = sem("small_constants")
        s_xps = sem("x_transposed")
        s_xT = sem("xT_in_sbuf")
        s_conv = sem("conv_products")
        s_h = sem("h_in_sbuf")
        s_bst = sem("batch_stats")
        s_bagg = sem("bn_chain")
        s_bpow = sem("bn_rstd")
        s_bn = sem("bn_affine_ready")
        s_full = sem("job_done")
        s_drain = sem("job_copied_out")
        s_hb = sem("h_normalised")
        s_lst = sem("ln_stats_done")
        s_lmv = sem("ln_mv_done")
        s_lve = sem("ln_var_eps")
        s_lpow = sem("ln_power")
        s_lrs = sem("ln_rstd_done")
        s_xn = sem("xn_ready")
        s_yn = sem("yn_ready")
        s_nmax = sem("attn_max")
        s_prob = sem("attn_probs")
        s_rinv = sem("attn_inverse")
        s_h2 = sem("h2_tiles")
        s_resid = sem("residual_with_bias")
        s_y2a = sem("pos_conv_step1")
        s_y2b = sem("pos_conv_step2")
        s_y2 = sem("y2T_ready")
        s_p1 = sem("qk_part1")
        s_rem = sem("qk_remainder")
        s_p2 = sem("qk_part2")
        s_p3 = sem("qk_part3")
        s_seen = sem("parts_seen")
        s_v = sem("values_ready")
        s_stack = [sem(f"stack{u}_loaded") for u in range(2)]
        s_vh = sem("v_head_ready")
        s_sc = sem("scores_ready")
        s_ta = sem("top_a_found")
        s_rest = sem("rest_ready")
        s_tb = sem("top_b_found")
        s_shift = sem("shift_ready")
        s_pen = sem("penalty_ready")
        s_st = sem("masked_scoresT")
        s_wT = sem("weightsT_ready")
        s_pv = sem("head_output")
        s_o = sem("o_raw_ready")
        s_oinv = sem("o_inverse")
        s_on = sem("o_normalised")
        s_res = sem("result_ready")
        s_out = sem("result_stored")

        def halves(ap):
            return ap.rearrange("p (h n) -> p h n", h=2)

        def copied(eng, number):
            eng.wait_ge(s_drain, number + 1)

        def periods(eng_period, eng):
            for j in range(FIRST, TPB):
                eng_period(-1, j, front=0)
            for j in range(FIRST):
                eng_period(0, j, front=None)
            with eng.Fori(0, B - 1) as b:
                for j in range(FIRST, LAST_PERIOD):
                    eng_period(b, j, front=b + 1)
            for j in range(FIRST, LAST_PERIOD):
                eng_period(B - 1, j, front=None)

        def begun(b):
            return not (isinstance(b, int) and b < 0)

        def steps(b, j, lag):
            i = j - lag
            if isinstance(b, int) and (b < 0 or (b == 0 and i < 0) or (b == B - 1 and i >= TPB)):
                return None, None
            return i, b * TPB + i

        def apart(ins):
            return ins.wait_op(s_id0, 2, "sem-ge")

        block = ctx.enter_context(nc.Block())

        @block.sync
        def _(sp):
            for dst, src in (
                (W_rows[:], tok_W.rearrange("o (c f) -> o c f", c=TAPS)),
                (Wq_sb[:], attn_Wq), (Wk_sb[:], attn_Wk),
                (qkv_rows[:], qkv_w.rearrange("(j o) i -> o j i", j=3)),
                (wo_rows[:], wo_w),
                (posw[:], pos_w.rearrange("c a k -> c (a k)")),
                (vb_row[:], qkv_b[2 * C:3 * C].partition_broadcast(P)),
                (wob_row[:], wo_b.partition_broadcast(P)),
            ):
                sp.dma_start(dst, src).then_inc(s_w, 16)
            for j in range(2):
                sp.dma_start(qkvb[:, j, :], qkv_b[C * j:C * (j + 1)].rearrange("(p a) -> p a", a=1)).then_inc(s_w, 16)
            for i, v in enumerate((tok_b, tok_gamma, tok_beta, attn_bq, attn_bk, pos_b)):
                sp.dma_start(vec[:, i:i + 1], v.rearrange("(p a) -> p a", a=1)).then_inc(s_w, 16)

            for u in range(2):
                sp.dma_start(x_sb[0:XR, u], x[u].rearrange("(t p) f -> p t f", p=XR)).then_inc(s_xin[u], 16)
            with sp.Fori(1, B // 2) as p:
                for u in range(2):
                    sp.wait_ge(s_xps, 2 * p + u - 1)
                    sp.dma_start(x_sb[0:XR, u], x[2 * p + u].rearrange("(t p) f -> p t f", p=XR)
                                 ).then_inc(s_xin[u], 16)

            def load_stack(b, h):
                u, fb = h % 2, b + h // HEADS
                if h % HEADS == 0:
                    sp.wait_ge(s_p1, 2 * fb + 2)
                    sp.wait_ge(s_p2, 2 * fb + 2)
                    sp.wait_ge(s_p3, 2 * fb + 2)
                    sp.sem_inc(s_seen, 1)
                if not (isinstance(b, int) and b == 0 and h < 2):
                    sp.wait_ge(s_st, b * TPB + NT * (h - 1))
                c = D * (h % HEADS)
                for g in range(8):
                    i, j = g // 3, g % 3
                    sp.dma_start(stack[D * g:D * g + D, u, 0, :], parts[c:c + D, 0, i, :]).then_inc(s_stack[u], 16)
                    sp.dma_start(stack[D * g:D * g + D, u, 1, :], parts[c:c + D, 1, j, :]).then_inc(s_stack[u], 16)

            def batch(b):
                for h in range(2, HEADS if isinstance(b, int) else HEADS + 2):
                    load_stack(b, h)
                sp.wait_ge(s_res, 2 * b + 2)
                sp.dma_start(out[b, 0:(NT - 1) * P, :].rearrange("(t p) c -> p t c", p=P), res[:, 0:NT - 1, :]
                             ).then_inc(s_out, 16)
                sp.dma_start(out[b, (NT - 1) * P:N, :], res[0:LAST, NT - 1, :]).then_inc(s_out, 16)

            sp.sem_inc(s_out, 16)
            load_stack(0, 0)
            load_stack(0, 1)
            with sp.Fori(0, B - 1) as b:
                batch(b)
            batch(B - 1)
            sp.wait_ge(s_out, 32 * B + 16)

        @block.gpsimd
        def _(pool):
            nc.gpsimd.memset(ident[:], 0.0).then_inc(s_id0, 1)
            nc.gpsimd.memset(neg_ident[:], 0.0).then_inc(s_id0, 1)
            nc.gpsimd.memset(neg_big[:], 0.0).then_inc(s_id0, 1)
            pool.wait_ge(s_id0, 3)
            nc.gpsimd.affine_select(out=neg_big[:], in_=neg_big[:], compare_op=ALU.not_equal, fill=-BIG,
                                    base=0, pattern=[[-1, P]], channel_multiplier=1).then_inc(s_id, 1)
            nc.gpsimd.affine_select(out=ident[:], in_=ident[:], compare_op=ALU.not_equal, fill=1.0,
                                    base=0, pattern=[[-1, P]], channel_multiplier=1).then_inc(s_id, 1)
            nc.gpsimd.affine_select(out=neg_ident[:], in_=neg_ident[:], compare_op=ALU.not_equal, fill=-1.0,
                                    base=0, pattern=[[-1, P]], channel_multiplier=1).then_inc(s_id, 1)
            nc.gpsimd.memset(ones_bf[:], 1.0).then_inc(s_mem, 1)
            nc.gpsimd.memset(real[:], 1.0).then_inc(s_mem, 1)
            nc.gpsimd.memset(neg_half[:], -0.5).then_inc(s_mem, 1)
            nc.gpsimd.memset(hb[:, N:NP], 0.0).then_inc(s_mem, 1)
            nc.gpsimd.memset(qT[:, N:NP], 0.0).then_inc(s_mem, 1)
            nc.gpsimd.memset(prob[:, N:NP], 0.0).then_inc(s_mem, 1)
            nc.gpsimd.memset(yT[:, 0:1], 0.0).then_inc(s_mem, 1)
            nc.gpsimd.memset(y2T[:, N:NP], 0.0).then_inc(s_mem, 1)
            nc.gpsimd.memset(parts[:, :, :, N:NP], 0.0).then_inc(s_mem, 1)
            nc.gpsimd.memset(pen[:, :, N:NP], 1.0).then_inc(s_mem, 1)
            nc.gpsimd.memset(v_aug[:, :, :, D:DA], 1.0).then_inc(s_mem, 1)
            pool.wait_ge(s_mem, 11)
            nc.gpsimd.affine_select(out=real[:], in_=real[:], compare_op=ALU.is_ge, fill=0.0, base=N - 1,
                                    pattern=[[-P, NT]], channel_multiplier=-1).then_inc(s_mem, 1)
            pool.wait_ge(s_w, 16 * WEIGHT_LOADS)
            nc.gpsimd.tensor_scalar(bq_s[:], vec[:, 3:4], SCALE, None, ALU.mult).then_inc(s_small, 1)
            nc.gpsimd.tensor_scalar(q2b_s[:], qkvb[:, 0, :], SCALE, None, ALU.mult).then_inc(s_small, 1)
            nc.gpsimd.tensor_scalar(posw1[:], posw[:, 1:2], 1.0, None, ALU.add).then_inc(s_small, 1)
            pool.wait_ge(s_bagg, 2)
            nc.gpsimd.tensor_tensor(tok_rstd[:], tok_ve[:], neg_half[:, 0:1], ALU.pow).then_inc(s_bpow, 1)

            pool.wait_ge(s_mem, 12)
            pool.wait_ge(s_small, 3)

            def front_ops(j, fb):
                for ln, at in ((0, 11), (1, 37)):
                    if j == at:
                        pool.wait_ge(s_lmv, NT * (2 * fb + ln + 1))
                        apart(nc.gpsimd.tensor_scalar(ln_ve[:], ln_mv[:, :, 1], EPS, None, ALU.add)).then_inc(s_lve, 1)
                        pool.wait_ge(s_lve, 2 * fb + ln + 1)
                        nc.gpsimd.tensor_tensor(ln_pow[:], ln_ve[:], neg_half[:], ALU.pow).then_inc(s_lpow, 1)
                        pool.wait_ge(s_lpow, 2 * fb + ln + 1)
                        nc.gpsimd.tensor_tensor(ln_rstd[:], ln_pow[:], real[:], ALU.mult).then_inc(s_lrs, 1)
                if 20 <= j <= 35 and (j - 20) % 3 == 0:
                    t = (j - 20) // 3
                    copied(pool, front_no(fb, f"A0.{t}"))
                    nc.gpsimd.tensor_tensor(h2[:, t, :], att[:], h1[:, t, :], ALU.add).then_inc(s_h2, 1)
                if j == 38:
                    pool.wait_ge(s_h2, NT * fb + NT)
                    for t in range(NT):
                        nc.gpsimd.tensor_tensor(hT[:, fb, P * t:P * (t + 1)], h2[:, t, :], wob_row[:], ALU.add
                                                ).then_inc(s_resid, 1)
                for w, name, at in ((0, "qh1", 43), (1, "kh1", 44)):
                    if j == at:
                        copied(pool, front_no(fb, name))
                        pool.wait_ge(s_p1, 2 * fb + w + 1)
                        nc.gpsimd.tensor_tensor(rem[:, w, :], qf[:, w, :], parts[:, w, 0, 0:N], ALU.subtract
                                                ).then_inc(s_rem, 1)
                    if j == at + 1:
                        pool.wait_ge(s_rem, 2 * fb + w + 1)
                        pool.wait_ge(s_p2, 2 * fb + w + 1)
                        nc.gpsimd.tensor_tensor(parts[:, w, 2, 0:N], rem[:, w, :], parts[:, w, 1, 0:N], ALU.subtract
                                                ).then_inc(s_p3, 1)
                if j in (46, 47):
                    f = j - 46
                    copied(pool, front_no(fb, "v1"))
                    for t in range(3 * f, 3 * f + 3):
                        nc.gpsimd.tensor_tensor(v_aug[:, t, :, 0:D], v_rows[:, t, :].rearrange("p (h d) -> p h d", d=D),
                                                vb_row[:].rearrange("p (h d) -> p h d", d=D), ALU.add).then_inc(s_v, 1)

            def period(b, j, front):
                i, n = steps(b, j, 1)
                if i is not None:
                    s = i % 2
                    if i % NT == 0:
                        u = (i // NT) % 2
                        if i % TPB == 0:
                            pool.wait_ge(s_v, NT * (b + i // TPB + 1))
                        if not (isinstance(b, int) and b == 0 and i < 2 * NT):
                            pool.wait_ge(s_pv, n - NT)
                        apart(nc.gpsimd.tensor_copy(v_head[:, u, :, :], v_aug[:, :, (i // NT) % HEADS, :])
                              ).then_inc(s_vh, 1)
                    pool.wait_ge(s_ta, n + 1)
                    if not (isinstance(b, int) and b == 0 and i < 2):
                        pool.wait_ge(s_st, n - 1)
                    apart(nc.gpsimd.tensor_scalar(shift[:, s, :], neg_ident[:], top_a[:, s, 0:1], 1.0,
                                                  ALU.mult, ALU.mult)).then_inc(s_shift, 1)
                if front is not None:
                    front_ops(j, front)
                if begun(b) and j in (55,):
                    copied(pool, end_no(b, "out1"))
                    pool.wait_ge(s_out, 32 * b + 16)
                    for f in range(2):
                        nc.gpsimd.tensor_tensor(res[:, 3 * f:3 * f + 3, :].rearrange("p t c -> p (t c)"),
                                                proj[:, 3 * f:3 * f + 3, :].rearrange("p t c -> p (t c)"),
                                                hT[:, b, 3 * P * f:3 * P * (f + 1)], ALU.add).then_inc(s_res, 1)

            periods(period, pool)

        @block.tensor
        def _(pe):
            def mm(o, l, r, start=True, stop=True):
                return nc.tensor.matmul(o, lhsT=l, rhs=r, start=start, stop=stop, skip_group_check=True)

            pe.wait_ge(s_w, 16 * WEIGHT_LOADS)
            pe.wait_ge(s_id, 3)
            for c in range(TAPS):
                last = nc.tensor.transpose(pair[0][:, c // 3, P * (c % 3):P * (c % 3 + 1)], W_rows[:, c, :], ident[:])
            last.then_inc(s_wt, 1)
            for j in range(3):
                nc.tensor.transpose(pair[1][:, 0, P * j:P * (j + 1)], qkv_rows[:, j, :], ident[:])
            nc.tensor.transpose(pair[1][:, 1, 0:P], wo_rows[:], ident[:]).then_inc(s_wt, 1)
            pe.wait_ge(s_wc, 4)

            def tok(p, first):
                for u in range(2):
                    pe.wait_ge(s_xin[u], 16 * (p + 1))
                    if not first:
                        pe.wait_ge(s_xT, 2 * p + u - 1)
                    for t in range(NT):
                        last = nc.tensor.transpose(pair[u][:, t // 3, XR * (t % 3):XR * (t % 3 + 1)],
                                                   x_sb[0:XR, u, t, :], ident[0:XR, 0:XR])
                    last.then_inc(s_xps, 1)
                for u in range(2):
                    pe.wait_ge(s_xT, 2 * p + u + 1)
                    if not first:
                        pe.wait_ge(s_h, 2 * p + u - 1)
                    for f in range(2):
                        for c in range(TAPS):
                            last = mm(pair[2 + u][:, f, 0:H2], W_cols[:, c, :], xT[:, u, H2 * f + c:H2 * f + c + H2],
                                      c == 0, c == TAPS - 1)
                    last.then_inc(s_conv, 1)

            tok(0, True)
            with pe.Fori(1, B // 2) as p:
                tok(p, False)
            pe.wait_ge(s_xT, B)
            pe.wait_ge(s_h, B)

            bank = pair[3][:, 0, :]
            obank = pair[3][:, 1, 0:DA]

            def turn(blocks, src):
                for n, t in enumerate(blocks):
                    last = nc.tensor.transpose(bank[:, P * n:P * (n + 1)], src(t), ident[:])
                return last

            HALF = (range(0, 4), range(4, NT))

            def job(b, j, slot, front):
                if front is not None and (j, slot) in FRONT:
                    name, fb = FRONT[j, slot], front
                    number = front_no(fb, name)
                elif begun(b) and (j, slot) in END:
                    name, fb = END[j, slot], b
                    number = end_no(b, name)
                else:
                    return
                if not (isinstance(number, int) and number == 0):
                    pe.wait_ge(s_drain, number)
                kind = name.split(".")[0][:-1]
                half = int(name.split(".")[0][-1])
                t = int(name.split(".")[1]) if "." in name else None
                tokens = slice(H2 * half, H2 * (half + 1))
                if kind == "h_rows":
                    pe.wait_ge(s_hb, fb + 1)
                    last = turn(HALF[half], lambda t: hb[:, P * t:P * (t + 1)])
                elif kind == "xn_cols":
                    pe.wait_ge(s_xn, fb + 1)
                    last = turn(HALF[half], lambda t: xn[:, t, :])
                elif kind == "q":
                    last = mm(bank[:, 0:H2], Wq_sb[:], xnT[:, tokens])
                elif kind == "k":
                    last = mm(bank[:, 0:H2], Wk_sb[:], xnT[:, tokens])
                elif kind == "S":
                    last = mm(bank[:, 0:H2], qT[:, P * t:P * (t + 1)], kT[:, tokens])
                elif kind == "P":
                    pe.wait_ge(s_prob, NT * fb + t + 1)
                    last = turn(HALF[half], lambda j: prob[:, P * j:P * (j + 1)])
                elif kind == "A":
                    for k in range(NT):
                        last = mm(bank[:, 0:P], probT[:, k, :], xn[:, k, :], k == 0, k == NT - 1)
                elif kind == "y_cols":
                    pe.wait_ge(s_yn, fb + 1)
                    last = turn(HALF[half], lambda t: yn[:, t, :])
                elif kind in ("qh", "kh"):
                    pe.wait_ge(s_y2, fb + 1)
                    last = mm(bank[:, 0:H2], qkv_cols[:, ("qh", "kh").index(kind), :], y2T[:, tokens])
                elif kind == "v":
                    for n, k in enumerate(HALF[half]):
                        last = mm(bank[:, P * n:P * (n + 1)], y2T[:, P * k:P * (k + 1)], qkv_cols[:, 2, :])
                elif kind == "o_cols":
                    pe.wait_ge(s_on, fb + 1)
                    last = turn(HALF[half], lambda t: o_n[:, t, :, :].rearrange("p h d -> p (h d)"))
                elif kind == "out":
                    for n, k in enumerate(HALF[half]):
                        last = mm(bank[:, P * n:P * (n + 1)], oT[:, P * k:P * (k + 1)], wo_cols[:])
                last.then_inc(s_full, 1)

            def period(b, j, front):
                i, n = steps(b, j, 0)
                if i is not None:
                    s, u = i % 2, (i // NT) % 2
                    if i % NT == 0:
                        pe.wait_ge(s_stack[u], 256 * (b * (HEADS // 2) + i // (2 * NT) + 1))
                    if not (isinstance(b, int) and b == 0 and i < 2):
                        pe.wait_ge(s_pen, n - 1)
                    for f in range(2):
                        last = mm(pair[s][:, f, 0:H2], stack[:, u, 0, P * (i % NT):P * (i % NT + 1)],
                                  stack[:, u, 1, H2 * f:H2 * (f + 1)])
                    last.then_inc(s_sc, 1)
                job(b, j, "F", front)
                i, n = steps(b, j, 2)
                if i is not None:
                    s, u = i % 2, (i // NT) % 2
                    pe.wait_ge(s_shift, n + 1)
                    pe.wait_ge(s_pen, n + 1)
                    if not (isinstance(b, int) and b == 0 and i < 1):
                        pe.wait_ge(s_wT, n)
                    for f in range(2):
                        o = pair[2][:, f, :]
                        mm(o[:, 0:3 * P].rearrange("p (j q) -> p j q", j=3), ones_bf[:],
                           shift[:, s:s + 1, :].broadcast_to([P, 3, P]), True, False)
                        for k in range(3):
                            keys = slice(P * (3 * f + k), P * (3 * f + k + 1))
                            dst = o[:, P * k:P * (k + 1)]
                            mm(dst, stack[:, u, 1, keys], stack[:, u, 0, P * (i % NT):P * (i % NT + 1)], False, False)
                            last = mm(dst, pen[:, s, keys], neg_big[:], False, k == 2)
                    last.then_inc(s_st, 1)
                job(b, j, "G", front)
                i, n = steps(b, j, 3)
                if i is not None:
                    s, u = i % 2, (i // NT) % 2
                    if i % NT == 0:
                        pe.wait_ge(s_vh, b * HEADS + i // NT + 1)
                    pe.wait_ge(s_wT, n + 1)
                    if not (isinstance(b, int) and b == 0 and i < 1):
                        pe.wait_ge(s_o, n)
                    for k in range(NT):
                        last = mm(obank, wT[:, s, k // 3, P * (k % 3):P * (k % 3 + 1)], v_head[:, u, k, :],
                                  k == 0, k == NT - 1)
                    last.then_inc(s_pv, 1)

            periods(period, pe)

        @block.scalar
        def _(act):
            act.wait_ge(s_wt, 2)
            nc.scalar.activation(W_cols[:, 0:3, :], pair[0][:, 0, 0:3 * P], ACT.Copy).then_inc(s_wc, 1)
            nc.scalar.activation(W_cols[:, 3:TAPS, :], pair[0][:, 1, 0:(TAPS - 3) * P], ACT.Copy).then_inc(s_wc, 1)
            nc.scalar.activation(qkv_cols[:], pair[1][:, 0, 0:3 * P], ACT.Copy).then_inc(s_wc, 1)
            nc.scalar.activation(wo_cols[:], pair[1][:, 1, 0:P], ACT.Copy).then_inc(s_wc, 1)

            def tok(p, first):
                for u in range(2):
                    act.wait_ge(s_xps, 2 * p + u + 1)
                    if not first:
                        act.wait_ge(s_conv, 2 * p + u - 1)
                    nc.scalar.activation(halves(xT[:, u, :]), pair[u][:, :, 0:T // 2], ACT.Copy).then_inc(s_xT, 1)
                for u in range(2):
                    act.wait_ge(s_conv, 2 * p + u + 1)
                    nc.scalar.activation(halves(hT[:, 2 * p + u, 0:N]), pair[2 + u][:, :, 0:H2], ACT.Relu,
                                         bias=vec[:, 0:1]).then_inc(s_h, 1)

            tok(0, True)
            with act.Fori(1, B // 2) as p:
                tok(p, False)
            act.wait_ge(s_bn, 1)
            act.wait_ge(s_small, 3)
            act.wait_ge(s_mem, 11)

            act.wait_ge(s_mem, 12)
            bank = pair[3][:, 0, :]

            def copy_out(b, j, slot, front):
                if front is not None and (j, slot) in FRONT:
                    name, fb = FRONT[j, slot], front
                    number = front_no(fb, name)
                elif begun(b) and (j, slot) in END:
                    name, fb = END[j, slot], b
                    number = end_no(b, name)
                else:
                    return
                act.wait_ge(s_full, number + 1)
                kind = name.split(".")[0][:-1]
                half = int(name.split(".")[0][-1])
                t = int(name.split(".")[1]) if "." in name else None
                tokens = slice(H2 * half, H2 * (half + 1))
                tiles = slice(4 * half, min(4 * half + 4, NT))
                width = P * (4, 2)[half]
                at = 4 * P * half
                wide, product = bank[:, 0:width], bank[:, 0:H2]
                if kind == "h_rows":
                    ins = nc.scalar.activation(h1[:, tiles, :], wide, ACT.Copy)
                elif kind == "xn_cols":
                    ins = nc.scalar.activation(xnT[:, at:at + width], wide, ACT.Copy)
                elif kind == "q":
                    ins = nc.scalar.activation(qT[:, tokens], product, ACT.Identity, bias=bq_s[:], scale=SCALE)
                elif kind == "k":
                    ins = nc.scalar.activation(kT[:, tokens], product, ACT.Identity, bias=vec[:, 4:5])
                elif kind == "S":
                    ins = nc.scalar.activation(att_sc[:, tokens], product, ACT.Copy)
                elif kind == "P":
                    ins = nc.scalar.activation(probT[:, tiles, :], wide, ACT.Copy)
                elif kind == "A":
                    act.wait_ge(s_rinv, NT * fb + t + 1)
                    if not (isinstance(fb, int) and t == 0):
                        act.wait_ge(s_h2, NT * fb + t)
                    ins = nc.scalar.activation(att[:], bank[:, 0:P], ACT.Copy, scale=row_inv[:])
                elif kind == "y_cols":
                    ins = nc.scalar.activation(yT[:, 1 + at:1 + at + width], wide, ACT.Copy)
                elif kind == "qh":
                    ins = nc.scalar.activation(qf[:, 0, tokens], product, ACT.Identity, bias=q2b_s[:], scale=SCALE)
                elif kind == "kh":
                    ins = nc.scalar.activation(qf[:, 1, tokens], product, ACT.Identity, bias=qkvb[:, 1, :])
                elif kind == "v":
                    ins = nc.scalar.activation(v_rows[:, tiles, :], wide, ACT.Copy)
                elif kind == "o_cols":
                    ins = nc.scalar.activation(oT[:, at:at + width], wide, ACT.Copy)
                elif kind == "out":
                    ins = nc.scalar.activation(proj[:, tiles, :], wide, ACT.Copy)
                ins.then_inc(s_drain, 1)

            def period(b, j, front):
                i, n = steps(b, j, 2)
                if i is not None:
                    s = i % 2
                    act.wait_ge(s_tb, n + 1)
                    if not (isinstance(b, int) and b == 0 and i < 2):
                        act.wait_ge(s_st, n - 1)
                    nc.scalar.activation(halves(pen[:, s, 0:N]), pair[s][:, :, 0:H2], ACT.Relu,
                                         bias=top_b[:, s, 7:8], scale=-1.0).then_inc(s_pen, 1)
                i, n = steps(b, j, 3)
                if i is not None:
                    act.wait_ge(s_st, n + 1)
                    if not (isinstance(b, int) and b == 0 and i < 2):
                        act.wait_ge(s_pv, n - 1)
                    nc.scalar.activation(wT[:, i % 2], pair[2][:, :, 0:3 * P], ACT.Exp).then_inc(s_wT, 1)
                copy_out(b, j, "F", front)
                i, n = steps(b, j, 4)
                if i is not None:
                    h = (i // NT) % HEADS
                    act.wait_ge(s_pv, n + 1)
                    nc.scalar.activation(o_raw[:, b + i // TPB, i % NT, DA * h:DA * (h + 1)],
                                         pair[3][:, 1, 0:DA], ACT.Copy).then_inc(s_o, 1)
                copy_out(b, j, "G", front)
                if front is not None and j == FIRST:
                    nc.scalar.activation(hb[:, 0:N], hT[:, front, 0:N], ACT.Identity, bias=bn_bias[:],
                                         scale=bn_scale[:]).then_inc(s_hb, 1)
                if front is not None and 17 <= j <= 32 and (j - 17) % 3 == 0:
                    t = (j - 17) // 3
                    act.wait_ge(s_nmax, NT * front + t + 1)
                    nc.scalar.activation(prob[:, 0:N], att_sc[:], ACT.Exp, bias=neg_max[:],
                                         accum_out=row_sum[:]).then_inc(s_prob, 1)

            periods(period, act)

        @block.vector
        def _(dve):
            with dve.Fori(0, B // 2) as p:
                for u in range(2):
                    dve.wait_ge(s_h, 2 * p + u + 1)
                    for f in range(2):
                        nc.vector.bn_stats(stats[:, 2 * p + u, f, :], hT[:, 2 * p + u, H2 * f:H2 * (f + 1)]
                                           ).then_inc(s_bst, 1)
            dve.wait_ge(s_bst, 2 * B)
            nc.vector.bn_aggr(tok_mv[:], stats[:].rearrange("p b f s -> p (b f s)")).then_inc(s_bagg, 1)
            dve.wait_ge(s_bagg, 1)
            nc.vector.tensor_scalar(tok_ve[:], tok_mv[:, 1:2], EPS, None, ALU.add).then_inc(s_bagg, 1)
            dve.wait_ge(s_bpow, 1)
            dve.wait_ge(s_w, 16 * WEIGHT_LOADS)
            nc.vector.tensor_tensor(bn_scale[:], tok_rstd[:], vec[:, 1:2], ALU.mult).then_inc(s_bagg, 1)
            dve.wait_ge(s_bagg, 3)
            nc.vector.tensor_tensor(bn_tmp[:], tok_mv[:, 0:1], bn_scale[:], ALU.mult).then_inc(s_bagg, 1)
            dve.wait_ge(s_bagg, 4)
            nc.vector.tensor_tensor(bn_bias[:], vec[:, 2:3], bn_tmp[:], ALU.subtract).then_inc(s_bn, 1)
            dve.wait_ge(s_small, 3)

            def front_ops(j, slot, fb):
                at = j, slot
                for ln, src, dst, stats_at, mv_at, out_at, done in (
                        (0, h1, xn, {(10, "a"): (0, 1, 2), (10, "b"): (3, 4, 5)}, {(11, "a"): range(NT)}, 12, s_xn),
                        (1, h2, yn, {(21 + 3 * t, "b"): (t,) for t in range(NT)},
                         {(22 + 3 * t, "a"): (t,) for t in range(NT)}, 38, s_yn)):
                    for t in stats_at.get(at, ()):
                        if ln == 0:
                            if t in (0, 3):
                                copied(dve, front_no(fb, "h_rows1"))
                        else:
                            dve.wait_ge(s_h2, NT * fb + t + 1)
                        nc.vector.bn_stats(ln_stats[:, t, :], src[:, t, :]).then_inc(s_lst, 1)
                    for t in mv_at.get(at, ()):
                        dve.wait_ge(s_lst, NT * (2 * fb + ln) + t + 1)
                        apart(nc.vector.bn_aggr(ln_mv[:, t, :], ln_stats[:, t, :])).then_inc(s_lmv, 1)
                    if j == out_at:
                        if slot == "a":
                            dve.wait_ge(s_lmv, NT * (2 * fb + ln + 1))
                            dve.wait_ge(s_lrs, 2 * fb + ln + 1)
                        for t in range(3 * (slot == "b"), 3 * (slot == "b") + 3):
                            last = nc.vector.tensor_scalar(dst[:, t, :], src[:, t, :], ln_mv[:, t, 0:1],
                                                           ln_rstd[:, t:t + 1], ALU.subtract, ALU.mult)
                        if slot == "b":
                            last.then_inc(done, 1)
                if slot == "a" and 17 <= j <= 32 and (j - 17) % 3 == 0:
                    t = (j - 17) // 3
                    copied(dve, front_no(fb, f"S1.{t}"))
                    nc.vector.tensor_reduce(neg_max[:], att_sc[:], AX.X, ALU.max, negate=True).then_inc(s_nmax, 1)
                if slot == "a" and 18 <= j <= 33 and (j - 18) % 3 == 0:
                    t = (j - 18) // 3
                    dve.wait_ge(s_prob, NT * fb + t + 1)
                    nc.vector.reciprocal(row_inv[:], row_sum[:]).then_inc(s_rinv, 1)
                if at == (40, "a"):
                    copied(dve, front_no(fb, "y_cols1"))
                    nc.vector.tensor_scalar(y2a[:], yT[:, 1:N + 1], posw1[:], vec[:, 5:6], ALU.mult, ALU.add
                                            ).then_inc(s_y2a, 1)
                if at == (40, "b"):
                    dve.wait_ge(s_y2a, fb + 1)
                    nc.vector.scalar_tensor_tensor(y2b[:], yT[:, 0:N], posw[:, 0:1], y2a[:], ALU.mult, ALU.add
                                                   ).then_inc(s_y2b, 1)
                if at == (41, "a"):
                    dve.wait_ge(s_y2b, fb + 1)
                    nc.vector.scalar_tensor_tensor(y2T[:, 0:N], yT[:, 2:N + 2], posw[:, 2:3], y2b[:],
                                                   ALU.mult, ALU.add).then_inc(s_y2, 1)
                for w, name, one, two in ((0, "qh1", (43, "a"), (44, "b")), (1, "kh1", (44, "a"), (45, "a"))):
                    if at == one:
                        copied(dve, front_no(fb, name))
                        if w == 0 and not isinstance(fb, int):
                            for u in range(2):
                                dve.wait_ge(s_stack[u], 256 * (HEADS // 2) * fb)
                        nc.vector.tensor_copy(parts[:, w, 0, 0:N], qf[:, w, :]).then_inc(s_p1, 1)
                    if at == two:
                        dve.wait_ge(s_rem, 2 * fb + w + 1)
                        nc.vector.tensor_copy(parts[:, w, 1, 0:N], rem[:, w, :]).then_inc(s_p2, 1)

            def period(b, j, front):
                i, n = steps(b, j, 1)
                started = not (isinstance(b, int) and b == 0 and i is not None and i < 2)
                if i is not None:
                    s = i % 2
                    scores = pair[s][:, :, 0:H2]
                    dve.wait_ge(s_sc, n + 1)
                    if started:
                        dve.wait_ge(s_shift, n - 1)
                    apart(nc.vector.max(top_a[:, s, :], scores)).then_inc(s_ta, 1)
                if front is not None:
                    front_ops(j, "a", front)
                if begun(b) and j == 52:
                    dve.wait_ge(s_o, (b + 1) * TPB)
                    nc.vector.reciprocal(o_inv[:].rearrange("p t h -> p (t h)"),
                                         o_raw[:, b].rearrange("p t (h d) -> p (t h) d", d=DA)[:, :, D]
                                         ).then_inc(s_oinv, 1)
                if i is not None:
                    dve.wait_ge(s_ta, n + 1)
                    apart(nc.vector.match_replace(rest[:], top_a[:, s, :], scores, -3.0e38)).then_inc(s_rest, 1)
                if front is not None:
                    front_ops(j, "b", front)
                if begun(b) and j == 52:
                    dve.wait_ge(s_oinv, b + 1)
                    nc.vector.tensor_tensor(o_n[:].rearrange("p t h d -> p (t h) d"),
                                            o_raw[:, b].rearrange("p t (h d) -> p (t h) d", d=DA)[:, :, 0:D],
                                            o_inv[:].rearrange("p t h -> p (t h)").unsqueeze(2).broadcast_to(
                                                [P, NT * HEADS, D]), ALU.mult).then_inc(s_on, 1)
                if i is not None:
                    dve.wait_ge(s_rest, n + 1)
                    if started:
                        dve.wait_ge(s_pen, n - 1)
                    apart(nc.vector.max(top_b[:, s, :], rest[:])).then_inc(s_tb, 1)

            periods(period, dve)


_INS = ['x', 'L0_tok_W', 'L0_tok_b', 'L0_tok_gamma', 'L0_tok_beta', 'L0_attn_Wq', 'L0_attn_bq', 'L0_attn_Wk',
        'L0_attn_bk', 'L0_ffn_pos_w', 'L0_ffn_pos_b', 'L0_ffn_qkv_w', 'L0_ffn_qkv_b', 'L0_ffn_wo_w', 'L0_ffn_wo_b']
_OUTS = [((8, 746, 128), 'float32')]


def kernel(**inputs):
    import numpy as _np
    import concourse.bacc as _bacc
    from concourse import mybir as _mybir
    from concourse.bass_utils import run_bass_kernel_spmd as _run

    nc = _bacc.Bacc("TRN2", target_bir_lowering=False, num_devices=1)
    arrays, args = {}, []
    for name in _INS:
        a = _np.ascontiguousarray(inputs[name])
        arrays[f"in_{name}_dram"] = a
        args.append(nc.dram_tensor(f"in_{name}_dram", a.shape, _mybir.dt.from_np(a.dtype), kind="ExternalInput").ap())
    for i, (shape, dtype) in enumerate(_OUTS):
        dt = _mybir.dt.from_np(_np.dtype(dtype))
        args.append(nc.dram_tensor(f"out_{i}_dram", shape, dt, kind="ExternalOutput").ap())
    audio_tower_kernel(nc, *args)
    r = _run(nc, [arrays], core_ids=[0])
    got = tuple(r.results[0][f"out_{i}_dram"] for i in range(len(_OUTS)))
    return got[0]
```

```python
from contextlib import ExitStack

import concourse.bass as bass
from concourse import mybir

P = 128
F32 = mybir.dt.float32
BF16 = mybir.dt.bfloat16
ALU = mybir.AluOpType
ACT = mybir.ActivationFunctionType
AX = mybir.AxisListType

STEPS = 48
FIRST, LAST_PERIOD = 8, 56
START = 0
S0_AT = ((10, "G"), (14, "F"), (18, "F"), (22, "F"), (26, "F"), (29, "F"))
S1_AT = ((11, "F"), (14, "G"), (18, "G"), (22, "G"), (26, "G"), (29, "G"))
MAX_AT = ((12, "b"), (16, "a"), (20, "a"), (24, "a"), (28, "a"), (31, "a"))
EXP_AT = (12, 16, 20, 24, 28, 31)
P_AT = (13, 17, 21, 25, 30, 32)
A_AT = (16, 20, 24, 28, 31, 34)
Y_AT = A_AT[-1] + 2
FRONT = {(1, "F"): "h_rows0", (1, "G"): "h_rows1", (7, "F"): "xn_cols0", (8, "G"): "xn_cols1",
         (8, "F"): "q0", (9, "F"): "k0", (9, "G"): "q1", (10, "F"): "k1",
         (Y_AT + 2, "F"): "y_cols0", (Y_AT + 2, "G"): "y_cols1", (Y_AT + 5, "F"): "qh0", (Y_AT + 5, "G"): "qh1",
         (Y_AT + 6, "F"): "kh0", (Y_AT + 6, "G"): "kh1", (Y_AT + 8, "F"): "v0", (Y_AT + 9, "F"): "v1"}
for _t in range(6):
    for _at, _name in ((S0_AT[_t], "S0"), (S1_AT[_t], "S1"), ((P_AT[_t], "F"), "P0"), ((P_AT[_t], "G"), "P1"),
                       ((A_AT[_t], "F"), "A0")):
        assert _at not in FRONT
        FRONT[_at] = f"{_name}.{_t}"
END = {(53, "F"): "o_cols0", (53, "G"): "o_cols1", (54, "F"): "out0", (54, "G"): "out1"}
NEEDS = {"q0": "xn_cols0", "k0": "xn_cols0", "q1": "xn_cols1", "k1": "xn_cols1", "S0.0": "k0", "S1.0": "k1",
         "out0": "o_cols0", "out1": "o_cols1"} | {f"A0.{_t}": f"P1.{_t}" for _t in range(6)}
SLOT = {name: slot for (_, slot), name in (FRONT | END).items()}


def in_turn(jobs):
    return {name: n for n, (_, name) in enumerate(sorted(jobs.items()))}


TURN = END | {(j if j >= FIRST else j + STEPS, slot): name for (j, slot), name in FRONT.items()}
EARLY = {name for (j, _), name in FRONT.items() if j < FIRST}
assert len(TURN) == len(FRONT) + len(END) and all(j < STEPS - 1 for j, _ in FRONT)
FRONT_NO, TURN_NO, END_NO = in_turn(FRONT), in_turn(TURN), in_turn(END)


def jobs_since(name, slot=None, first_front=False):
    if first_front:
        return FRONT_NO[name] - FRONT_NO[NEEDS[name]]
    turn = list(TURN_NO)
    found = []
    for jobs in ([turn + turn] + ([turn + list(END_NO)] if name in END_NO else [])):
        at = len(jobs) - 1 - jobs[::-1].index(name)
        found += [at - n for n in range(at) if (SLOT[jobs[n]] == slot if slot else jobs[n] == NEEDS[name])]
    return min(found)


def audio_tower_kernel(nc: bass.Bass, x, tok_W, tok_b, tok_gamma, tok_beta, attn_Wq, attn_bq, attn_Wk, attn_bk,
                       pos_w, pos_b, qkv_w, qkv_b, wo_w, wo_b, out):
    B, T, C = x.shape
    TAPS = tok_W.shape[1] // C
    N = T - TAPS + 1
    H2 = N // 2
    NT = -(-N // P)
    NP = NT * P
    LAST = N - (NT - 1) * P
    XR = T // NT
    HEADS = 8
    D = C // HEADS
    DA = D + 1
    SCALE = float(C) ** -0.5
    EPS = 1e-5
    WEIGHT_LOADS = 14
    TPB = HEADS * NT
    BIG = float(2.0 ** 80)
    assert TPB == STEPS and N == 2 * H2 and XR * NT == T and C == P and H2 <= 512 and NT == 6 and B % 2 == 0

    PAIRS = ((0, 0), (0, 1), (0, 2), (1, 0), (1, 1), (2, 0))
    RQ = len(PAIRS) * D
    NF, NE = len(FRONT), len(END)
    qk_parts = nc.dram_tensor("qk_parts", [B, 2, 3, C, NP], BF16, kind="Internal").ap()

    def front_no(fb, name):
        if first(fb):
            return FRONT_NO[name]
        return (NF + NE) * fb + len(EARLY) + TURN_NO[name] - (NF + NE if name in EARLY else 0)

    def end_no(b, name):
        place = END_NO[name] if isinstance(b, int) and b == B - 1 else TURN_NO[name]
        return (NF + NE) * b + NF + len(EARLY) + NE + place

    def first(fb):
        return isinstance(fb, int) and fb == 0

    with ExitStack() as ctx:
        def sb(name, shape, dt=F32):
            return ctx.enter_context(nc.sbuf_tensor(name, shape, dt))

        def sem(name):
            return ctx.enter_context(nc.semaphore(name))

        pair = [ctx.enter_context(nc.psum_tensor(f"pair{i}", [P, 2, 512], F32)) for i in range(4)]

        ident = sb("ident", [P, P])
        ident_bf = sb("ident_bf", [P, P], BF16)
        neg_big = sb("neg_big", [P, P], BF16)
        W_rows = sb("W_rows", [P, TAPS, P])
        W_cols = sb("W_cols", [P, TAPS, P])
        Wq_sb = sb("Wq_sb", [P, P])
        Wk_sb = sb("Wk_sb", [P, P])
        qkv_rows = sb("qkv_rows", [P, 3, P])
        qkv_cols = sb("qkv_cols", [P, 3, P])
        wo_rows = sb("wo_rows", [P, P])
        wo_cols = sb("wo_cols", [P, P])
        vec = sb("vec", [P, 6])
        qkvb = sb("qkvb", [P, 2, 1])
        posw = sb("posw", [P, 3])
        vb_row = sb("vb_row", [P, C])
        wob_row = sb("wob_row", [P, C])
        bq_s = sb("bq_s", [P, 1])
        q2b_s = sb("q2b_s", [P, 1])
        posw1 = sb("posw1", [P, 1])
        real = sb("real", [P, NT])
        neg_half = sb("neg_half", [P, NT])

        x_sb = sb("x_sb", [P, 2, NT, P])
        xT = sb("xT", [P, 2, T])
        hT = sb("hT", [P, B + 1, NP])
        stats = sb("stats", [P, B, 2, 6])
        tok_mv = sb("tok_mv", [P, 2])
        tok_ve = sb("tok_ve", [P, 1])
        tok_rstd = sb("tok_rstd", [P, 1])
        bn_scale = sb("bn_scale", [P, 1])
        bn_tmp = sb("bn_tmp", [P, 1])
        bn_bias = sb("bn_bias", [P, 1])

        hb = sb("hb", [P, NP])
        h1 = sb("h1", [P, NT, P])
        h2 = sb("h2", [P, NT, P])
        ln_stats = sb("ln_stats", [P, NT, 6])
        ln_mv = sb("ln_mv", [P, NT, 2])
        ln_ve = sb("ln_ve", [P, NT])
        ln_pow = sb("ln_pow", [P, NT])
        ln_rstd = sb("ln_rstd", [P, NT])
        xn = sb("xn", [P, NT, P])
        xnT = sb("xnT", [P, NP])
        qT = sb("qT", [P, NP])
        kT = sb("kT", [P, N])
        att_sc = sb("att_sc", [P, N])
        neg_max = sb("neg_max", [P, 1])
        prob = sb("prob", [P, NP])
        row_sum = sb("row_sum", [P, 1])
        row_inv = sb("row_inv", [P, 2])
        probT = sb("probT", [P, NT, P])
        att = sb("att", [P, P])
        yn = sb("yn", [P, NT, P])
        yT = sb("yT", [P, NP + 1])
        y2a = sb("y2a", [P, N])
        y2b = sb("y2b", [P, N])
        y2T = sb("y2T", [P, NP])
        qf = sb("qf", [P, 2, N])
        rem = sb("rem", [P, 2, N])
        parts = sb("parts", [P, 2, 3, NP], BF16)
        v_rows = sb("v_rows", [P, NT, P])
        v_aug = sb("v_aug", [P, B, NT, HEADS, DA])

        stack = sb("stack", [P, 2, 2, NP], BF16)
        top_a = sb("top_a", [P, 2, 8])
        top_b = sb("top_b", [P, 2, 8])
        rest = sb("rest", [P, 2, H2])
        shift = sb("shift", [P, 2, RQ + 2], BF16)
        pen = sb("pen", [P, 2, NP], BF16)
        wT = sb("wT", [P, 2, 2, 3 * P])
        o_raw = sb("o_raw", [P, B, NT, HEADS * DA])
        o_inv = sb("o_inv", [P, NT, HEADS])
        o_n = sb("o_n", [P, NT, HEADS, D])
        oT = sb("oT", [P, NP])
        proj = sb("proj", [P, NT, P])
        res = sb("res", [P, NT, P])

        s_w_tok = sem("tokenizer_weights_loaded")
        s_w = sem("other_weights_loaded")
        s_xin = [sem(f"x_loaded{u}") for u in range(2)]
        s_mem = sem("memsets_done")
        s_id0 = sem("ident_zeroed")
        s_id = sem("ident_ready")
        s_wt = sem("weight_transposes")
        s_wc = sem("weight_copies")
        s_small = sem("small_constants")
        s_xps = sem("x_transposed")
        s_xT = sem("xT_in_sbuf")
        s_conv = sem("conv_products")
        s_h = sem("h_in_sbuf")
        s_bst = sem("batch_stats")
        s_bagg = sem("bn_chain")
        s_bpow = sem("bn_rstd")
        s_bn = sem("bn_affine_ready")
        s_full = sem("job_done")
        s_drain = sem("job_copied_out")
        s_hb = sem("h_normalised")
        s_lst = sem("ln_stats_done")
        s_lmv = sem("ln_mv_done")
        s_lve = sem("ln_var_eps")
        s_lpow = sem("ln_power")
        s_lrs = sem("ln_rstd_done")
        s_xn = sem("xn_ready")
        s_yn = sem("yn_ready")
        s_nmax = sem("attn_max")
        s_prob = sem("attn_probs")
        s_rinv = sem("attn_inverse")
        s_h2 = sem("h2_tiles")
        s_resid = sem("residual_with_bias")
        s_y2a = sem("pos_conv_step1")
        s_y2b = sem("pos_conv_step2")
        s_y2 = sem("y2T_ready")
        s_p1 = sem("qk_part1")
        s_rem = sem("qk_remainder")
        s_p2 = sem("qk_part2")
        s_p3 = sem("qk_part3")
        s_q_stored = sem("q_parts_in_dram")
        s_k01_stored = sem("k_parts_0_and_1_in_dram")
        s_k2_stored = sem("k_part_2_in_dram")
        s_seen = sem("parts_seen")
        s_v = sem("values_ready")
        s_stack = [sem(f"stack{u}_loaded") for u in range(2)]
        s_sc = sem("scores_ready")
        s_ta = sem("top_a_found")
        s_rest = sem("rest_ready")
        s_tb = sem("top_b_found")
        s_shift = sem("shift_ready")
        s_ones = sem("constant_rows_set")
        s_shift1 = sem("shift_part1")
        s_row = sem("shift_rows")
        s_rowc = sem("shift_rows_in_stack")
        s_pen = sem("penalty_ready")
        s_st = sem("masked_scoresT")
        s_wT = sem("weightsT_ready")
        s_pv = sem("head_output")
        s_o = sem("o_raw_ready")
        s_oinv = sem("o_inverse")
        s_on = sem("o_normalised")
        s_res = sem("result_ready")
        s_out = sem("result_stored")

        def halves(ap):
            return ap.rearrange("p (h n) -> p h n", h=2)

        def stored(w, part):
            return (s_q_stored, 48) if w == 0 else (s_k01_stored, 32) if part < 2 else (s_k2_stored, 16)

        def parts_free(eng, w, part, fb):
            if not first(fb):
                sem, each = stored(w, part)
                eng.wait_ge(sem, each * fb)

        def copied(eng, number):
            eng.wait_ge(s_drain, number + 1)

        def periods(eng_period, eng):
            for j in range(START, TPB):
                eng_period(-1, j, front=0)
            for j in range(FIRST):
                eng_period(0, j, front=1)
            with eng.Fori(0, B - 1) as b:
                for j in range(FIRST, LAST_PERIOD):
                    eng_period(b, j, front=b + 1 + j // TPB)
            for j in range(FIRST, LAST_PERIOD):
                eng_period(B - 1, j, front=None)

        def begun(b):
            return not (isinstance(b, int) and b < 0)

        def steps(b, j, lag):
            i = j - lag
            if isinstance(b, int) and (b < 0 or (b == 0 and i < 0) or (b == B - 1 and i >= TPB)):
                return None, None
            return i, b * TPB + i

        def job_at(b, j, slot, front):
            if front is not None and (j % TPB, slot) in FRONT:
                name = FRONT[j % TPB, slot]
                return name, front, front_no(front, name)
            if begun(b) and (j, slot) in END:
                return END[j, slot], b, end_no(b, END[j, slot])
            if isinstance(b, int) and b == 0 and (j + TPB, slot) in END:
                return "none", None, end_no(-1, END[j + TPB, slot])
            return None, None, None

        def front_before(b, j, front):
            return B if isinstance(b, int) and b == B - 1 and j == FIRST else front

        def job_bank(b, name):
            if not begun(b):
                return pair[FRONT_NO[name] // 2 % 2][:, FRONT_NO[name] % 2, :], 4
            return pair[3][:, "FG".index(SLOT[name]), :], jobs_since(name, slot=SLOT[name])

        def values_from(h):
            return max(0, DA * (h + 1) - P)

        def apart(ins):
            return ins.wait_op(s_id0, 2, "sem-ge")

        block = ctx.enter_context(nc.Block())

        @block.sync
        def _(sp):
            sp.dma_start(W_rows[:], tok_W.rearrange("o (c f) -> o c f", c=TAPS)).then_inc(s_w_tok, 16)
            for u in range(2):
                sp.dma_start(x_sb[0:XR, u], x[u].rearrange("(t p) f -> p t f", p=XR)).then_inc(s_xin[u], 16)
            sp.dma_start(vec[:, 0:1], tok_b.rearrange("(p a) -> p a", a=1)).then_inc(s_w_tok, 16)
            for dst, src in (
                (qkv_rows[:], qkv_w.rearrange("(j o) i -> o j i", j=3)),
                (wo_rows[:], wo_w),
                (Wq_sb[:], attn_Wq), (Wk_sb[:], attn_Wk),
                (posw[:], pos_w.rearrange("c a k -> c (a k)")),
                (vb_row[:], qkv_b[2 * C:3 * C].partition_broadcast(P)),
                (wob_row[:], wo_b.partition_broadcast(P)),
            ):
                sp.dma_start(dst, src).then_inc(s_w, 16)
            for j in range(2):
                sp.dma_start(qkvb[:, j, :], qkv_b[C * j:C * (j + 1)].rearrange("(p a) -> p a", a=1)).then_inc(s_w, 16)
            for i, v in enumerate((tok_gamma, tok_beta, attn_bq, attn_bk, pos_b)):
                sp.dma_start(vec[:, i + 1:i + 2], v.rearrange("(p a) -> p a", a=1)).then_inc(s_w, 16)

            with sp.Fori(1, B // 2) as p:
                for u in range(2):
                    sp.wait_ge(s_xps, 2 * p + u - 1)
                    sp.dma_start(x_sb[0:XR, u], x[2 * p + u].rearrange("(t p) f -> p t f", p=XR)
                                 ).then_inc(s_xin[u], 16)

            def store_parts(fb):
                for part, ready, each in ((0, s_p1, 2), (1, s_p2, 1), (2, s_p3, 1)):
                    for w in range(2):
                        sp.wait_ge(ready, each * (2 * fb + w + 1))
                        sp.dma_start(qk_parts[fb, w, part], parts[:, w, part, :]).then_inc(stored(w, part)[0], 16)

            def load_stack(b, h):
                u, fb = h % 2, b + h // HEADS
                if not (isinstance(b, int) and b == 0 and h < 2):
                    sp.wait_ge(s_st, b * TPB + NT * (h - 1))
                c = D * (h % HEADS)

                def wait_stored(w, part):
                    if h % HEADS == 0:
                        sem, each = stored(w, part)
                        sp.wait_ge(sem, each * (fb + 1))
                        sp.sem_inc(s_seen, 1)

                wait_stored(0, 0)
                for i, (row, times) in enumerate(((0, 3), (3, 2), (5, 1))):
                    sp.dma_start(stack[D * row:D * (row + times), u, 0, :],
                                 qk_parts[fb, 0, i:i + 1, c:c + D, :].broadcast_to([times, D, NP])
                                 ).then_inc(s_stack[u], 16)
                wait_stored(1, 0)
                for row, count in ((5, 1), (3, 2), (0, 3)):
                    if row == 0:
                        wait_stored(1, 2)
                    sp.dma_start(stack[D * row:D * (row + count), u, 1, :], qk_parts[fb, 1, 0:count, c:c + D, :]
                                 ).then_inc(s_stack[u], 16)

            def batch(b):
                for h in range(2, HEADS):
                    load_stack(b, h)
                if not isinstance(b, int):
                    store_parts(b + 1)
                    load_stack(b, HEADS)
                    load_stack(b, HEADS + 1)
                sp.wait_ge(s_res, 2 * b + 2)
                sp.dma_start(out[b, 0:(NT - 1) * P, :].rearrange("(t p) c -> p t c", p=P), res[:, 0:NT - 1, :]
                             ).then_inc(s_out, 16)
                sp.dma_start(out[b, (NT - 1) * P:N, :], res[0:LAST, NT - 1, :]).then_inc(s_out, 16)

            sp.sem_inc(s_out, 16)
            store_parts(0)
            load_stack(0, 0)
            load_stack(0, 1)
            with sp.Fori(0, B - 1) as b:
                batch(b)
            batch(B - 1)
            sp.wait_ge(s_out, 32 * B + 16)
            for w, part in ((0, 0), (1, 0), (1, 2)):
                sem, each = stored(w, part)
                sp.wait_ge(sem, each * B)

        @block.gpsimd
        def _(pool):
            nc.gpsimd.memset(ident[:], 0.0).then_inc(s_id0, 1)
            nc.gpsimd.memset(ident_bf[:], 0.0).then_inc(s_id0, 1)
            nc.gpsimd.memset(neg_big[:], 0.0).then_inc(s_id0, 1)
            pool.wait_ge(s_id0, 3)
            nc.gpsimd.affine_select(out=neg_big[:], in_=neg_big[:], compare_op=ALU.not_equal, fill=-BIG,
                                    base=0, pattern=[[-1, P]], channel_multiplier=1).then_inc(s_id, 1)
            nc.gpsimd.affine_select(out=ident[:], in_=ident[:], compare_op=ALU.not_equal, fill=1.0,
                                    base=0, pattern=[[-1, P]], channel_multiplier=1).then_inc(s_id, 1)
            nc.gpsimd.affine_select(out=ident_bf[:], in_=ident_bf[:], compare_op=ALU.not_equal, fill=1.0,
                                    base=0, pattern=[[-1, P]], channel_multiplier=1).then_inc(s_id, 1)
            nc.gpsimd.memset(shift[:], 0.0).then_inc(s_mem, 1)
            nc.gpsimd.memset(real[:], 1.0).then_inc(s_mem, 1)
            nc.gpsimd.memset(neg_half[:], -0.5).then_inc(s_mem, 1)
            nc.gpsimd.memset(hb[:, N:NP], 0.0).then_inc(s_mem, 1)
            nc.gpsimd.memset(qT[:, N:NP], 0.0).then_inc(s_mem, 1)
            nc.gpsimd.memset(prob[:, N:NP], 0.0).then_inc(s_mem, 1)
            nc.gpsimd.memset(yT[:, 0:1], 0.0).then_inc(s_mem, 1)
            nc.gpsimd.memset(y2T[:, N:NP], 0.0).then_inc(s_mem, 1)
            nc.gpsimd.memset(parts[:, :, :, N:NP], 0.0).then_inc(s_mem, 1)
            nc.gpsimd.memset(pen[:, :, N:NP], 1.0).then_inc(s_mem, 1)
            nc.gpsimd.memset(v_aug[:, :, :, :, D:DA], 1.0).then_inc(s_mem, 1)
            pool.wait_ge(s_mem, 11)
            nc.gpsimd.affine_select(out=real[:], in_=real[:], compare_op=ALU.is_ge, fill=0.0, base=N - 1,
                                    pattern=[[-P, NT]], channel_multiplier=-1).then_inc(s_mem, 1)
            pool.wait_ge(s_w, 16 * WEIGHT_LOADS)
            nc.gpsimd.tensor_scalar(bq_s[:], vec[:, 3:4], SCALE, None, ALU.mult).then_inc(s_small, 1)
            nc.gpsimd.tensor_scalar(q2b_s[:], qkvb[:, 0, :], SCALE, None, ALU.mult).then_inc(s_small, 1)
            nc.gpsimd.tensor_scalar(posw1[:], posw[:, 1:2], 1.0, None, ALU.add).then_inc(s_small, 1)
            pool.wait_ge(s_bagg, 2)
            nc.gpsimd.tensor_tensor(tok_rstd[:], tok_ve[:], neg_half[:, 0:1], ALU.pow).then_inc(s_bpow, 1)

            pool.wait_ge(s_mem, 12)
            pool.wait_ge(s_small, 3)

            def front_ops(j, fb):
                for ln, at in ((0, 5), (1, Y_AT)):
                    if j == at:
                        pool.wait_ge(s_lmv, NT * (2 * fb + ln + 1))
                        apart(nc.gpsimd.tensor_scalar(ln_ve[:], ln_mv[:, :, 1], EPS, None, ALU.add)).then_inc(s_lve, 1)
                        pool.wait_ge(s_lve, 2 * fb + ln + 1)
                        nc.gpsimd.tensor_tensor(ln_pow[:], ln_ve[:], neg_half[:], ALU.pow).then_inc(s_lpow, 1)
                        pool.wait_ge(s_lpow, 2 * fb + ln + 1)
                        nc.gpsimd.tensor_tensor(ln_rstd[:], ln_pow[:], real[:], ALU.mult).then_inc(s_lrs, 1)
                if j - 1 in A_AT:
                    t = A_AT.index(j - 1)
                    copied(pool, front_no(fb, f"A0.{t}"))
                    nc.gpsimd.tensor_tensor(h2[:, t, :], att[:], h1[:, t, :], ALU.add).then_inc(s_h2, 1)
                if j == Y_AT + 3:
                    pool.wait_ge(s_h2, NT * fb + NT)
                    for t in range(NT):
                        nc.gpsimd.tensor_tensor(hT[:, fb, P * t:P * (t + 1)], h2[:, t, :], wob_row[:], ALU.add
                                                ).then_inc(s_resid, 1)
                for w, name, at in ((1, "kh1", Y_AT + 7), (0, "qh1", Y_AT + 6)):
                    if j == at:
                        copied(pool, front_no(fb, name))
                        nc.gpsimd.tensor_tensor(rem[:, w, :], qf[:, w, :], parts[:, w, 0, 0:N], ALU.subtract
                                                ).then_inc(s_rem, 1)
                    if j == at + 2:
                        pool.wait_ge(s_rem, 2 * fb + w + 1)
                        pool.wait_ge(s_p2, 2 * fb + w + 1)
                        parts_free(pool, w, 2, fb)
                        nc.gpsimd.tensor_tensor(parts[:, w, 2, 0:N], rem[:, w, :], parts[:, w, 1, 0:N], ALU.subtract
                                                ).then_inc(s_p3, 1)
                if j in (Y_AT + 10, Y_AT + 11):
                    f = j - Y_AT - 10
                    copied(pool, front_no(fb, f"v{f}"))
                    for t in range(3 * f, 3 * f + 3):
                        nc.gpsimd.tensor_tensor(v_aug[:, fb, t, :, 0:D], v_rows[:, t, :].rearrange("p (h d) -> p h d", d=D),
                                                vb_row[:].rearrange("p (h d) -> p h d", d=D), ALU.add).then_inc(s_v, 1)

            def period(b, j, front):
                i, n = steps(b, j, 1)
                if i is not None:
                    s = i % 2
                    pool.wait_ge(s_ta, n + 1)
                    if not (isinstance(b, int) and b == 0 and i < 2):
                        pool.wait_ge(s_row, n - 1)
                    apart(nc.gpsimd.tensor_copy(shift[:, s, RQ:RQ + 1], top_a[:, s, 0:1])).then_inc(s_shift1, 1)
                    pool.wait_ge(s_shift1, n + 1)
                    nc.gpsimd.tensor_tensor(shift[:, s, RQ + 1:RQ + 2], top_a[:, s, 0:1], shift[:, s, RQ:RQ + 1],
                                            ALU.subtract).then_inc(s_shift, 1)
                if front is not None:
                    front_ops(j % TPB, front)
                if begun(b) and j == 52:
                    pool.wait_ge(s_oinv, b + 1)
                    nc.gpsimd.tensor_tensor(o_n[:].rearrange("p t h d -> p (t h) d"),
                                            o_raw[:, b].rearrange("p t (h d) -> p (t h) d", d=DA)[:, :, 0:D],
                                            o_inv[:].rearrange("p t h -> p (t h)").unsqueeze(2).broadcast_to(
                                                [P, NT * HEADS, D]), ALU.mult).then_inc(s_on, 1)
                if begun(b) and j == 55:
                    copied(pool, end_no(b, "out1"))
                    pool.wait_ge(s_out, 32 * b + 16)
                    for f in range(2):
                        nc.gpsimd.tensor_tensor(res[:, 3 * f:3 * f + 3, :].rearrange("p t c -> p (t c)"),
                                                proj[:, 3 * f:3 * f + 3, :].rearrange("p t c -> p (t c)"),
                                                hT[:, b, 3 * P * f:3 * P * (f + 1)], ALU.add).then_inc(s_res, 1)

            periods(period, pool)

        @block.tensor
        def _(pe):
            def mm(o, l, r, start=True, stop=True):
                return nc.tensor.matmul(o, lhsT=l, rhs=r, start=start, stop=stop, skip_group_check=True)

            pe.wait_ge(s_w_tok, 32)
            pe.wait_ge(s_id, 3)
            for c in range(TAPS):
                last = nc.tensor.transpose(pair[0][:, c // 3, P * (c % 3):P * (c % 3 + 1)], W_rows[:, c, :], ident[:])
            last.then_inc(s_wt, 1)
            pe.wait_ge(s_wc, 2)

            def tok(p, first):
                for u in range(2):
                    pe.wait_ge(s_xin[u], 16 * (p + 1))
                    if not first:
                        pe.wait_ge(s_xT, 2 * p + u - 1)
                    for t in range(NT):
                        last = nc.tensor.transpose(pair[u][:, t // 3, XR * (t % 3):XR * (t % 3 + 1)],
                                                   x_sb[0:XR, u, t, :], ident[0:XR, 0:XR])
                    last.then_inc(s_xps, 1)
                for u in range(2):
                    pe.wait_ge(s_xT, 2 * p + u + 1)
                    if not first:
                        pe.wait_ge(s_h, 2 * p + u - 1)
                    for f in range(2):
                        for c in range(TAPS):
                            last = mm(pair[2 + u][:, f, 0:H2], W_cols[:, c, :], xT[:, u, H2 * f + c:H2 * f + c + H2],
                                      c == 0, c == TAPS - 1)
                    last.then_inc(s_conv, 1)

            tok(0, True)
            with pe.Fori(1, B // 2) as p:
                tok(p, False)
            pe.wait_ge(s_xT, B)
            pe.wait_ge(s_h, B)

            pe.wait_ge(s_w, 16 * WEIGHT_LOADS)
            for j in range(3):
                nc.tensor.transpose(pair[1][:, 0, P * j:P * (j + 1)], qkv_rows[:, j, :], ident[:])
            nc.tensor.transpose(pair[1][:, 1, 0:P], wo_rows[:], ident[:]).then_inc(s_wt, 1)
            pe.wait_ge(s_wc, 4)


            obank = pair[3][:, 1, 3 * P:4 * P]

            def turn(bank, blocks, src):
                for n, t in enumerate(blocks):
                    last = nc.tensor.transpose(bank[:, P * n:P * (n + 1)], src(t), ident[:])
                return last

            HALF = (range(0, 3), range(3, NT))

            def job(b, j, slot, front):
                name, fb, number = job_at(b, j, slot, front)
                if name is None:
                    return
                if name == "none":
                    pe.wait_ge(s_full, number)
                    pe.sem_inc(s_full, 1)
                    return
                kind = name.split(".")[0][:-1]
                bank, back = job_bank(b, name)
                i, n = steps(b, j, 4)
                if slot == "G" and i is not None:
                    pe.wait_ge(s_o, n + 1)
                if name in NEEDS:
                    back = min(back, jobs_since(name, first_front=not begun(b)))
                if not isinstance(number, int) or number >= back:
                    pe.wait_ge(s_drain, number - back + 1)
                half = int(name.split(".")[0][-1])
                t = int(name.split(".")[1]) if "." in name else None
                tokens = slice(H2 * half, H2 * (half + 1))
                if kind == "h_rows":
                    pe.wait_ge(s_hb, fb + 1)
                    last = turn(bank, HALF[half], lambda t: hb[:, P * t:P * (t + 1)])
                elif kind == "xn_cols":
                    pe.wait_ge(s_xn, NT * fb + 3 * half + 3)
                    last = turn(bank, HALF[half], lambda t: xn[:, t, :])
                elif kind == "q":
                    last = mm(bank[:, 0:H2], Wq_sb[:], xnT[:, tokens])
                elif kind == "k":
                    last = mm(bank[:, 0:H2], Wk_sb[:], xnT[:, tokens])
                elif kind == "S":
                    last = mm(bank[:, 0:H2], qT[:, P * t:P * (t + 1)], kT[:, tokens])
                elif kind == "P":
                    pe.wait_ge(s_prob, NT * fb + t + 1)
                    last = turn(bank, HALF[half], lambda j: prob[:, P * j:P * (j + 1)])
                elif kind == "A":
                    for k in range(NT):
                        last = mm(bank[:, 0:P], probT[:, k, :], xn[:, k, :], k == 0, k == NT - 1)
                elif kind == "y_cols":
                    pe.wait_ge(s_yn, NT * fb + 3 * half + 3)
                    last = turn(bank, HALF[half], lambda t: yn[:, t, :])
                elif kind in ("qh", "kh"):
                    pe.wait_ge(s_y2, fb + 1)
                    last = mm(bank[:, 0:H2], qkv_cols[:, ("qh", "kh").index(kind), :], y2T[:, tokens])
                elif kind == "v":
                    for n, k in enumerate(HALF[half]):
                        last = mm(bank[:, P * n:P * (n + 1)], y2T[:, P * k:P * (k + 1)], qkv_cols[:, 2, :])
                elif kind == "o_cols":
                    pe.wait_ge(s_on, fb + 1)
                    last = turn(bank, HALF[half], lambda t: o_n[:, t, :, :].rearrange("p h d -> p (h d)"))
                elif kind == "out":
                    for n, k in enumerate(HALF[half]):
                        last = mm(bank[:, P * n:P * (n + 1)], oT[:, P * k:P * (k + 1)], wo_cols[:])
                last.then_inc(s_full, 1)

            def period(b, j, front):
                i, n = steps(b, j, 0)
                if i is not None:
                    s, u = i % 2, (i // NT) % 2
                    if i % NT == 0:
                        pe.wait_ge(s_stack[u], 96 * (b * (HEADS // 2) + i // (2 * NT) + 1))
                    if isinstance(b, int) and b == 0 and i == 0:
                        pe.wait_ge(s_ones, 2)
                        pe.wait_ge(s_drain, NF)
                    if not (isinstance(b, int) and b == 0 and i < 2):
                        pe.wait_ge(s_pen, n - 1)
                    for f in range(2):
                        last = mm(pair[s][:, f, 0:H2], stack[0:RQ, u, 0, P * (i % NT):P * (i % NT + 1)],
                                  stack[0:RQ, u, 1, H2 * f:H2 * (f + 1)])
                    last.then_inc(s_sc, 1)
                i, n = steps(b, j, 2)
                if i is not None:
                    s, u = i % 2, (i // NT) % 2
                    pe.wait_ge(s_rowc, n + 1)
                    pe.wait_ge(s_pen, n + 1)
                    if not (isinstance(b, int) and b == 0 and i < 1):
                        pe.wait_ge(s_wT, n)
                    for f in range(2):
                        o = pair[2][:, f, :]
                        for k in range(3):
                            keys = slice(P * (3 * f + k), P * (3 * f + k + 1))
                            dst = o[:, P * k:P * (k + 1)]
                            mm(dst, stack[0:RQ + 2, u, 1, keys], stack[0:RQ + 2, u, 0, P * (i % NT):P * (i % NT + 1)],
                               True, False)
                            last = mm(dst, pen[:, s, keys], neg_big[:], False, True)
                    last.then_inc(s_st, 1)
                i, n = steps(b, j, 1)
                if i is not None:
                    pe.wait_ge(s_shift, n + 1)
                    pe.wait_ge(s_rest, n + 1)
                    mm(pair[i % 2][0:RQ + 2, 0, 3 * P:4 * P], shift[:, i % 2, :], ident_bf[:]).then_inc(s_row, 1)
                job(b, j, "F", front)
                job(b, j, "G", front)
                i, n = steps(b, j, 3)
                if i is not None:
                    s, u = i % 2, (i // NT) % 2
                    if i % TPB == 0:
                        pe.wait_ge(s_v, NT * (b + i // TPB + 1))
                    pe.wait_ge(s_wT, n + 1)
                    if not (isinstance(b, int) and b == 0 and i < 1):
                        pe.wait_ge(s_o, n)
                    name, _, number = job_at(b, j - 1, "G", front_before(b, j, front))
                    if name is not None:
                        copied(pe, number)
                    first = values_from((i // NT) % HEADS)
                    for k in range(NT):
                        last = mm(obank, wT[:, s, k // 3, P * (k % 3):P * (k % 3 + 1)], 
                                  v_aug[:, b + i // TPB, k, :, :].rearrange("p h d -> p (h d)")[:, first:first + P],
                                  k == 0, k == NT - 1)
                    last.then_inc(s_pv, 1)

            periods(period, pe)

        @block.scalar
        def _(act):
            act.wait_ge(s_wt, 1)
            nc.scalar.activation(W_cols[:, 0:3, :], pair[0][:, 0, 0:3 * P], ACT.Copy).then_inc(s_wc, 1)
            nc.scalar.activation(W_cols[:, 3:TAPS, :], pair[0][:, 1, 0:(TAPS - 3) * P], ACT.Copy).then_inc(s_wc, 1)

            def tok(p, first):
                for u in range(2):
                    act.wait_ge(s_xps, 2 * p + u + 1)
                    if not first:
                        act.wait_ge(s_conv, 2 * p + u - 1)
                    nc.scalar.activation(halves(xT[:, u, :]), pair[u][:, :, 0:T // 2], ACT.Copy).then_inc(s_xT, 1)
                for u in range(2):
                    act.wait_ge(s_conv, 2 * p + u + 1)
                    nc.scalar.activation(halves(hT[:, 2 * p + u, 0:N]), pair[2 + u][:, :, 0:H2], ACT.Relu,
                                         bias=vec[:, 0:1]).then_inc(s_h, 1)

            tok(0, True)
            with act.Fori(1, B // 2) as p:
                tok(p, False)
            act.wait_ge(s_wt, 2)
            nc.scalar.activation(qkv_cols[:], pair[1][:, 0, 0:3 * P], ACT.Copy).then_inc(s_wc, 1)
            nc.scalar.activation(wo_cols[:], pair[1][:, 1, 0:P], ACT.Copy).then_inc(s_wc, 1)
            act.wait_ge(s_bn, 1)
            act.wait_ge(s_small, 3)
            act.wait_ge(s_mem, 12)
            act.wait_ge(s_ones, 2)

            def copy_out(b, j, slot, front):
                name, fb, number = job_at(b, j, slot, front)
                if name is None:
                    return
                act.wait_ge(s_full, number + 1)
                if name == "none":
                    act.wait_ge(s_drain, number)
                    act.sem_inc(s_drain, 1)
                    return
                bank, _ = job_bank(b, name)
                kind = name.split(".")[0][:-1]
                half = int(name.split(".")[0][-1])
                t = int(name.split(".")[1]) if "." in name else None
                tokens = slice(H2 * half, H2 * (half + 1))
                tiles = slice(3 * half, 3 * half + 3)
                width = 3 * P
                at = width * half
                wide, product = bank[:, 0:width], bank[:, 0:H2]
                if kind == "h_rows":
                    ins = nc.scalar.activation(h1[:, tiles, :], wide, ACT.Copy)
                elif kind == "xn_cols":
                    ins = nc.scalar.activation(xnT[:, at:at + width], wide, ACT.Copy)
                elif kind == "q":
                    ins = nc.scalar.activation(qT[:, tokens], product, ACT.Identity, bias=bq_s[:], scale=SCALE)
                elif kind == "k":
                    ins = nc.scalar.activation(kT[:, tokens], product, ACT.Identity, bias=vec[:, 4:5])
                elif kind == "S":
                    if half == 0 and not (first(fb) and t == 0):
                        act.wait_ge(s_prob, NT * fb + t)
                    ins = nc.scalar.activation(att_sc[:, tokens], product, ACT.Copy)
                elif kind == "P":
                    ins = nc.scalar.activation(probT[:, tiles, :], wide, ACT.Copy)
                elif kind == "A":
                    act.wait_ge(s_rinv, NT * fb + t + 1)
                    if not (first(fb) and t == 0):
                        act.wait_ge(s_h2, NT * fb + t)
                    ins = nc.scalar.activation(att[:], bank[:, 0:P], ACT.Copy, scale=row_inv[:, t % 2:t % 2 + 1])
                elif kind == "y_cols":
                    ins = nc.scalar.activation(yT[:, 1 + at:1 + at + width], wide, ACT.Copy)
                elif kind == "qh":
                    parts_free(act, 0, 0, fb)
                    nc.scalar.activation(parts[:, 0, 0, tokens], product, ACT.Identity, bias=q2b_s[:], scale=SCALE
                                         ).then_inc(s_p1, 1)
                    ins = nc.scalar.activation(qf[:, 0, tokens], product, ACT.Identity, bias=q2b_s[:], scale=SCALE)
                elif kind == "kh":
                    parts_free(act, 1, 0, fb)
                    nc.scalar.activation(parts[:, 1, 0, tokens], product, ACT.Identity, bias=qkvb[:, 1, :]
                                         ).then_inc(s_p1, 1)
                    ins = nc.scalar.activation(qf[:, 1, tokens], product, ACT.Identity, bias=qkvb[:, 1, :])
                elif kind == "v":
                    ins = nc.scalar.activation(v_rows[:, tiles, :], wide, ACT.Copy)
                elif kind == "o_cols":
                    ins = nc.scalar.activation(oT[:, at:at + width], wide, ACT.Copy)
                elif kind == "out":
                    ins = nc.scalar.activation(proj[:, tiles, :], wide, ACT.Copy)
                ins.then_inc(s_drain, 1)

            def period(b, j, front):
                i, n = steps(b, j, 2)
                if i is not None:
                    act.wait_ge(s_row, n + 1)
                    nc.scalar.activation(stack[RQ:RQ + 2, (i // NT) % 2, 0, P * (i % NT):P * (i % NT + 1)],
                                         pair[i % 2][RQ:RQ + 2, 0, 3 * P:4 * P], ACT.Copy).then_inc(s_rowc, 1)
                i, n = steps(b, j, 2)
                if i is not None:
                    s = i % 2
                    act.wait_ge(s_tb, n + 1)
                    if not (isinstance(b, int) and b == 0 and i < 2):
                        act.wait_ge(s_st, n - 1)
                    nc.scalar.activation(halves(pen[:, s, 0:N]), pair[s][:, :, 0:H2], ACT.Relu,
                                         bias=top_b[:, s, 7:8], scale=-1.0).then_inc(s_pen, 1)
                copy_out(b, j - 1, "F", front_before(b, j, front))
                i, n = steps(b, j, 3)
                if i is not None:
                    act.wait_ge(s_st, n + 1)
                    if not (isinstance(b, int) and b == 0 and i < 2):
                        act.wait_ge(s_pv, n - 1)
                    nc.scalar.activation(wT[:, i % 2], pair[2][:, :, 0:3 * P], ACT.Exp).then_inc(s_wT, 1)
                i, n = steps(b, j, 4)
                if i is not None:
                    h = (i // NT) % HEADS
                    at = 3 * P + DA * h - values_from(h)
                    act.wait_ge(s_pv, n + 1)
                    nc.scalar.activation(o_raw[:, b + i // TPB, i % NT, DA * h:DA * (h + 1)],
                                         pair[3][:, 1, at:at + DA], ACT.Copy).then_inc(s_o, 1)
                copy_out(b, j - 1, "G", front_before(b, j, front))
                if front is not None and j % TPB == START:
                    nc.scalar.activation(hb[:, 0:N], hT[:, front, 0:N], ACT.Identity, bias=bn_bias[:],
                                         scale=bn_scale[:]).then_inc(s_hb, 1)
                if front is not None and j % TPB in EXP_AT:
                    t = EXP_AT.index(j % TPB)
                    act.wait_ge(s_nmax, NT * front + t + 1)
                    if not (first(front) and t == 0):
                        act.wait_ge(s_rinv, NT * front + t)
                    nc.scalar.activation(prob[:, 0:N], att_sc[:], ACT.Exp, bias=neg_max[:],
                                         accum_out=row_sum[:]).then_inc(s_prob, 1)
                if front is not None and j == Y_AT + 3:
                    copied(act, front_no(front, "y_cols1"))
                    nc.scalar.activation(y2a[:], yT[:, 1:N + 1], ACT.Identity, bias=vec[:, 5:6],
                                         scale=posw1[:]).then_inc(s_y2a, 1)

            periods(period, act)

        @block.vector
        def _(dve):
            nc.vector.memset(stack[RQ:RQ + 2, :, 1, :], -1.0).then_inc(s_ones, 1)
            nc.vector.memset(hT[:, B, 0:N], 0.0).then_inc(s_ones, 1)
            with dve.Fori(0, B // 2) as p:
                for u in range(2):
                    dve.wait_ge(s_h, 2 * p + u + 1)
                    for f in range(2):
                        nc.vector.bn_stats(stats[:, 2 * p + u, f, :], hT[:, 2 * p + u, H2 * f:H2 * (f + 1)]
                                           ).then_inc(s_bst, 1)
            dve.wait_ge(s_bst, 2 * B)
            nc.vector.bn_aggr(tok_mv[:], stats[:].rearrange("p b f s -> p (b f s)")).then_inc(s_bagg, 1)
            dve.wait_ge(s_bagg, 1)
            nc.vector.tensor_scalar(tok_ve[:], tok_mv[:, 1:2], EPS, None, ALU.add).then_inc(s_bagg, 1)
            dve.wait_ge(s_bpow, 1)
            dve.wait_ge(s_w, 16 * WEIGHT_LOADS)
            nc.vector.tensor_tensor(bn_scale[:], tok_rstd[:], vec[:, 1:2], ALU.mult).then_inc(s_bagg, 1)
            dve.wait_ge(s_bagg, 3)
            nc.vector.tensor_tensor(bn_tmp[:], tok_mv[:, 0:1], bn_scale[:], ALU.mult).then_inc(s_bagg, 1)
            dve.wait_ge(s_bagg, 4)
            nc.vector.tensor_tensor(bn_bias[:], vec[:, 2:3], bn_tmp[:], ALU.subtract).then_inc(s_bn, 1)
            dve.wait_ge(s_small, 3)

            def front_ops(j, slot, fb):
                at = j, slot
                for ln, src, stats_at, mv_at in (
                        (0, h1, {(2, "b"): (0,), (3, "a"): (1,), (3, "b"): (2,), (4, "a"): (3,), (4, "b"): (4,), (5, "a"): (5,)},
                         {(3, "a"): (0,), (3, "b"): (1,), (4, "a"): (2,), (4, "b"): (3,), (5, "a"): (4,), (5, "b"): (5,)}),
                        (1, h2, {(A_AT[t] + 1, "b"): (t,) for t in range(NT)},
                         {(A_AT[t] + 2, "a"): (t,) for t in range(NT)})):
                    for t in stats_at.get(at, ()):
                        if ln == 0:
                            if t in (0, 3):
                                copied(dve, front_no(fb, f"h_rows{t // 3}"))
                        else:
                            dve.wait_ge(s_h2, NT * fb + t + 1)
                        nc.vector.bn_stats(ln_stats[:, t, :], src[:, t, :]).then_inc(s_lst, 1)
                    for t in mv_at.get(at, ()):
                        dve.wait_ge(s_lst, NT * (2 * fb + ln) + t + 1)
                        apart(nc.vector.bn_aggr(ln_mv[:, t, :], ln_stats[:, t, :])).then_inc(s_lmv, 1)
                for ln, src, dst, out_at, done in (
                        (0, h1, xn, {(6, "a"): (0,), (6, "b"): (1,), (7, "a"): (2,), (7, "b"): (3,), (8, "a"): (4,),
                                      (8, "b"): (5,)}, s_xn),
                        (1, h2, yn, {(Y_AT + 1, "a"): (0, 1), (Y_AT + 1, "b"): (2, 3), (Y_AT + 2, "a"): (4, 5)}, s_yn)):
                    for t in out_at.get(at, ()):
                        if t == 0:
                            dve.wait_ge(s_lmv, NT * (2 * fb + ln + 1))
                            dve.wait_ge(s_lrs, 2 * fb + ln + 1)
                        nc.vector.tensor_scalar(dst[:, t, :], src[:, t, :], ln_mv[:, t, 0:1],
                                                ln_rstd[:, t:t + 1], ALU.subtract, ALU.mult).then_inc(done, 1)
                if at in MAX_AT:
                    t = MAX_AT.index(at)
                    copied(dve, front_no(fb, f"S1.{t}"))
                    nc.vector.tensor_reduce(neg_max[:], att_sc[:], AX.X, ALU.max, negate=True).then_inc(s_nmax, 1)
                if slot == "a" and j - 1 in EXP_AT:
                    t = EXP_AT.index(j - 1)
                    dve.wait_ge(s_prob, NT * fb + t + 1)
                    nc.vector.reciprocal(row_inv[:, t % 2:t % 2 + 1], row_sum[:]).then_inc(s_rinv, 1)
                if at == (Y_AT + 4, "a"):
                    dve.wait_ge(s_y2a, fb + 1)
                    nc.vector.scalar_tensor_tensor(y2b[:], yT[:, 0:N], posw[:, 0:1], y2a[:], ALU.mult, ALU.add
                                                   ).then_inc(s_y2b, 1)
                if at == (Y_AT + 4, "b"):
                    dve.wait_ge(s_y2b, fb + 1)
                    nc.vector.scalar_tensor_tensor(y2T[:, 0:N], yT[:, 2:N + 2], posw[:, 2:3], y2b[:],
                                                   ALU.mult, ALU.add).then_inc(s_y2, 1)
                for w, at_w in ((0, (Y_AT + 8, "a")), (1, (Y_AT + 9, "a"))):
                    if at == at_w:
                        dve.wait_ge(s_rem, 2 * fb + w + 1)
                        parts_free(dve, w, 1, fb)
                        nc.vector.tensor_copy(parts[:, w, 1, 0:N], rem[:, w, :]).then_inc(s_p2, 1)

            def period(b, j, front):
                i, n = steps(b, j, 1)
                started = not (isinstance(b, int) and b == 0 and i is not None and i < 2)
                if i is not None:
                    s = i % 2
                    scores = pair[s][:, :, 0:H2]
                    dve.wait_ge(s_sc, n + 1)
                    if started:
                        dve.wait_ge(s_shift, n - 1)
                    apart(nc.vector.max(top_a[:, s, :], scores)).then_inc(s_ta, 1)
                if front is not None:
                    front_ops(j % TPB, "a", front)
                if begun(b) and j == 52:
                    dve.wait_ge(s_o, (b + 1) * TPB)
                    nc.vector.reciprocal(o_inv[:].rearrange("p t h -> p (t h)"),
                                         o_raw[:, b].rearrange("p t (h d) -> p (t h) d", d=DA)[:, :, D]
                                         ).then_inc(s_oinv, 1)
                if i is not None:
                    dve.wait_ge(s_ta, n + 1)
                    apart(nc.vector.match_replace(rest[:], top_a[:, s, :], scores, -3.0e38)).then_inc(s_rest, 1)
                if front is not None:
                    front_ops(j % TPB, "b", front)
                if i is not None:
                    dve.wait_ge(s_rest, n + 1)
                    if started:
                        dve.wait_ge(s_pen, n - 1)
                    apart(nc.vector.max(top_b[:, s, :], rest[:])).then_inc(s_tb, 1)

            periods(period, dve)


_INS = ['x', 'L0_tok_W', 'L0_tok_b', 'L0_tok_gamma', 'L0_tok_beta', 'L0_attn_Wq', 'L0_attn_bq', 'L0_attn_Wk',
        'L0_attn_bk', 'L0_ffn_pos_w', 'L0_ffn_pos_b', 'L0_ffn_qkv_w', 'L0_ffn_qkv_b', 'L0_ffn_wo_w', 'L0_ffn_wo_b']
_OUTS = [((8, 746, 128), 'float32')]


def kernel(**inputs):
    import numpy as _np
    import concourse.bacc as _bacc
    from concourse import mybir as _mybir
    from concourse.bass_utils import run_bass_kernel_spmd as _run

    nc = _bacc.Bacc("TRN2", target_bir_lowering=False, num_devices=1)
    arrays, args = {}, []
    for name in _INS:
        a = _np.ascontiguousarray(inputs[name])
        arrays[f"in_{name}_dram"] = a
        args.append(nc.dram_tensor(f"in_{name}_dram", a.shape, _mybir.dt.from_np(a.dtype), kind="ExternalInput").ap())
    for i, (shape, dtype) in enumerate(_OUTS):
        dt = _mybir.dt.from_np(_np.dtype(dtype))
        args.append(nc.dram_tensor(f"out_{i}_dram", shape, dt, kind="ExternalOutput").ap())
    audio_tower_kernel(nc, *args)
    r = _run(nc, [arrays], core_ids=[0])
    got = tuple(r.results[0][f"out_{i}_dram"] for i in range(len(_OUTS)))
    return got[0]
```
